# Optimizing a Trainium2 kernel written in Bass

```python
import numpy as np
import jax
import jax.numpy as jnp

def _softmax(x, axis=-1):
    return jax.nn.softmax(x, axis=axis)

def _gelu(x):
    return jax.nn.gelu(x, approximate=True)

def _silu(x):
    return jax.nn.silu(x)

def _sigmoid(x):
    return jax.nn.sigmoid(x)

def _layernorm(x, axis=-1, eps=1e-05):
    m = jnp.mean(x, axis=axis, keepdims=True)
    v = jnp.var(x, axis=axis, keepdims=True)
    return (x - m) / jnp.sqrt(v + eps)

def _scatter_add(tgt, idx, src, axis=0):
    return tgt.at[idx].add(src)

def _segment_sum(src, seg, n):
    return jax.ops.segment_sum(src, seg, n)
kernel_name = 'mk_cond_seq_d4_seqx_r4_181039'

def setup_inputs(seed: int=0):
    np.random.seed(seed)
    _w = jnp.asarray

    def _rec_inputs():
        import jax
        import jax.numpy as jnp
        _rk = jax.random.key(seed)
        x = -0.0003482 + 1 * jax.random.normal(jax.random.fold_in(_rk, 1), (4, 512, 288), jnp.float32)
        _lenS = 512 - jax.random.randint(jax.random.fold_in(_rk, 7), (4,), 0, max(1, 512 // 4) + 1, jnp.int32)
        _lenS2 = 512 - jax.random.randint(jax.random.fold_in(_rk, 8), (4,), 0, max(1, 512 // 4) + 1, jnp.int32)
        cond_1152 = 0.00257642 + 1.0011 * jax.random.normal(jax.random.fold_in(_rk, 11), (4, 288), jnp.float32)
        return (x, cond_1152)
    x, cond_1152 = _rec_inputs()

    def _L0_cond_setup():
        import jax, jax.numpy as jnp
        import numpy as np
        from jax.scipy.linalg import expm
        N, D, COND_DIM = (288, 64, 288)
        B, T = (16, 256)

        def _rotation(cond, W, b):
            v = jax.nn.silu(cond) @ W.T + b
            iu, ju = jnp.triu_indices(D, k=1)
            A = jnp.zeros((cond.shape[0], D, D), dtype=v.dtype)
            A = A.at[:, iu, ju].set(v).at[:, ju, iu].set(-v)
            return expm(A)
        key = jax.random.key(seed)
        k1, k2, k3, k4, k5 = jax.random.split(key, 5)
        x = jax.random.normal(k1, (B, T, N), dtype=jnp.float32)
        cond = jax.random.normal(k2, (B, COND_DIM), dtype=jnp.float32)
        P = jax.random.normal(k3, (N, D), dtype=jnp.float32)
        n_skew = D * (D - 1) // 2
        bound = 1.0 / np.sqrt(COND_DIM)
        W = jax.random.uniform(k4, (n_skew, COND_DIM), minval=-bound, maxval=bound, dtype=jnp.float32)
        b = jax.random.uniform(k5, (n_skew,), minval=-bound, maxval=bound, dtype=jnp.float32)
        return {'x': x, 'cond': cond, 'P': P, 'W': W, 'b': b}
    _L0_cond_all = _L0_cond_setup()
    _L0_cond_in = {k: v for k, v in _L0_cond_all.items() if k in ('P', 'W', 'b')}
    del _L0_cond_all

    def _L1_cond_setup():
        import jax, jax.numpy as jnp
        import numpy as np
        B, L, C = (8, 256, 288)
        H = 16
        D = C // H
        FF = int(C * 4.0)
        EPS = 1e-06

        def _layernorm(x):
            mu = jnp.mean(x, axis=-1, keepdims=True)
            var = jnp.mean(jnp.square(x - mu), axis=-1, keepdims=True)
            return (x - mu) * jax.lax.rsqrt(var + EPS)

        def _modulate(x, shift, scale):
            return x * (1.0 + scale) + shift

        def _attention(h, W_qkv, b_qkv, W_proj, b_proj):
            b, l, c = h.shape
            qkv = h @ W_qkv + b_qkv
            qkv = qkv.reshape(b, l, 3, H, D)
            q, k, v = (qkv[:, :, 0], qkv[:, :, 1], qkv[:, :, 2])
            scale = D ** (-0.5)
            scores = jnp.einsum('blhd,bmhd->bhlm', q * scale, k)
            attn = jax.nn.softmax(scores, axis=-1)
            o = jnp.einsum('bhlm,bmhd->blhd', attn, v).reshape(b, l, c)
            return o @ W_proj + b_proj
        key = jax.random.key(seed)
        ks = jax.random.split(key, 12)
        s = 0.02
        return {'x': jax.random.normal(ks[0], (B, L, C), jnp.float32), 'c': jax.random.normal(ks[1], (B, 1, C), jnp.float32), 'W_qkv': jax.random.normal(ks[2], (C, 3 * C), jnp.float32) * s, 'b_qkv': jnp.zeros((3 * C,), jnp.float32), 'W_proj': jax.random.normal(ks[3], (C, C), jnp.float32) * s, 'b_proj': jnp.zeros((C,), jnp.float32), 'W_fc1': jax.random.normal(ks[4], (C, FF), jnp.float32) * s, 'b_fc1': jnp.zeros((FF,), jnp.float32), 'W_fc2': jax.random.normal(ks[5], (FF, C), jnp.float32) * s, 'b_fc2': jnp.zeros((C,), jnp.float32), 'W_ada': jax.random.normal(ks[6], (C, 6 * C), jnp.float32) * s, 'b_ada': jnp.zeros((6 * C,), jnp.float32)}
    _L1_cond_all = _L1_cond_setup()
    _L1_cond_in = {k: v for k, v in _L1_cond_all.items() if k in ('W_qkv', 'b_qkv', 'W_proj', 'b_proj', 'W_fc1', 'b_fc1', 'W_fc2', 'b_fc2', 'W_ada', 'b_ada')}
    del _L1_cond_all

    def _L2_cond_setup():
        import jax, jax.numpy as jnp
        import numpy as np
        HID = 288
        HEADS = 16
        HD = HID // HEADS
        MLP = int(HID * 4.0)

        def _ln(x, eps, gamma=None, beta=None):
            mu = jnp.mean(x, axis=-1, keepdims=True)
            var = jnp.mean(jnp.square(x - mu), axis=-1, keepdims=True)
            y = (x - mu) / jnp.sqrt(var + eps)
            if gamma is not None:
                y = y * gamma + beta
            return y
        key = jax.random.key(seed)
        ks = jax.random.split(key, 12)
        B, N, C = (8, 256, HID)
        s = lambda k, *sh: jax.random.normal(k, sh, dtype=jnp.float32) * 0.02
        return {'x': jax.random.normal(ks[0], (B, N, C), dtype=jnp.float32), 'c': jax.random.normal(ks[1], (B, C), dtype=jnp.float32), 'w_qkv': s(ks[2], C, 3 * C), 'b_qkv': jnp.zeros((3 * C,), jnp.float32), 'w_proj': s(ks[3], C, C), 'b_proj': jnp.zeros((C,), jnp.float32), 'qn_g': jnp.ones((HD,), jnp.float32), 'qn_b': jnp.zeros((HD,), jnp.float32), 'kn_g': jnp.ones((HD,), jnp.float32), 'kn_b': jnp.zeros((HD,), jnp.float32), 'w1': s(ks[4], C, MLP), 'b1': jnp.zeros((MLP,), jnp.float32), 'w2': s(ks[5], MLP, C), 'b2': jnp.zeros((C,), jnp.float32), 'w_ada': s(ks[6], C, 6 * C), 'b_ada': jnp.zeros((6 * C,), jnp.float32)}
    _L2_cond_all = _L2_cond_setup()
    _L2_cond_in = {k: v for k, v in _L2_cond_all.items() if k in ('w_qkv', 'b_qkv', 'w_proj', 'b_proj', 'qn_g', 'qn_b', 'kn_g', 'kn_b', 'w1', 'b1', 'w2', 'b2', 'w_ada', 'b_ada')}
    del _L2_cond_all

    def _L3_cond_setup():
        import jax, jax.numpy as jnp
        import numpy as np
        NUM_HEADS = 16
        NUM_EXPERTS = 4
        TOP_K = 2
        LN_EPS = 1e-06

        def _ln(h):
            mu = jnp.mean(h, axis=-1, keepdims=True)
            var = jnp.var(h, axis=-1, keepdims=True)
            return (h - mu) * jax.lax.rsqrt(var + LN_EPS)

        def _modulate(h, shift, scale):
            return h * (1.0 + scale[:, None, :]) + shift[:, None, :]
        key = jax.random.key(seed)
        ks = jax.random.split(key, 12)
        B, N, C = (8, 256, 288)
        H = 4 * C
        E = NUM_EXPERTS
        s = 0.02
        return {'x': jax.random.normal(ks[0], (B, N, C), jnp.float32), 'c': jax.random.normal(ks[1], (B, C), jnp.float32), 'w_adaln': jax.random.normal(ks[2], (C, 6 * C), jnp.float32) * s, 'b_adaln': jnp.zeros((6 * C,), jnp.float32), 'w_qkv': jax.random.normal(ks[3], (C, 3 * C), jnp.float32) * s, 'b_qkv': jnp.zeros((3 * C,), jnp.float32), 'w_proj': jax.random.normal(ks[4], (C, C), jnp.float32) * s, 'b_proj': jnp.zeros((C,), jnp.float32), 'w_gate': jax.random.normal(ks[5], (C, E), jnp.float32) * s, 'w1': jax.random.normal(ks[6], (E, C, H), jnp.float32) * s, 'b1': jnp.zeros((E, H), jnp.float32), 'w2': jax.random.normal(ks[7], (E, H, C), jnp.float32) * s, 'b2': jnp.zeros((E, C), jnp.float32)}
    _L3_cond_all = _L3_cond_setup()
    _L3_cond_in = {k: v for k, v in _L3_cond_all.items() if k in ('w_adaln', 'b_adaln', 'w_qkv', 'b_qkv', 'w_proj', 'b_proj', 'w_gate', 'w1', 'b1', 'w2', 'b2')}
    del _L3_cond_all
    return {'x': x, 'cond_1152': cond_1152, 'L0_cond_P': _L0_cond_in['P'], 'L0_cond_W': _L0_cond_in['W'], 'L0_cond_b': _L0_cond_in['b'], 'L1_cond_W_qkv': _L1_cond_in['W_qkv'], 'L1_cond_b_qkv': _L1_cond_in['b_qkv'], 'L1_cond_W_proj': _L1_cond_in['W_proj'], 'L1_cond_b_proj': _L1_cond_in['b_proj'], 'L1_cond_W_fc1': _L1_cond_in['W_fc1'], 'L1_cond_b_fc1': _L1_cond_in['b_fc1'], 'L1_cond_W_fc2': _L1_cond_in['W_fc2'], 'L1_cond_b_fc2': _L1_cond_in['b_fc2'], 'L1_cond_W_ada': _L1_cond_in['W_ada'], 'L1_cond_b_ada': _L1_cond_in['b_ada'], 'L2_cond_w_qkv': _L2_cond_in['w_qkv'], 'L2_cond_b_qkv': _L2_cond_in['b_qkv'], 'L2_cond_w_proj': _L2_cond_in['w_proj'], 'L2_cond_b_proj': _L2_cond_in['b_proj'], 'L2_cond_qn_g': _L2_cond_in['qn_g'], 'L2_cond_qn_b': _L2_cond_in['qn_b'], 'L2_cond_kn_g': _L2_cond_in['kn_g'], 'L2_cond_kn_b': _L2_cond_in['kn_b'], 'L2_cond_w1': _L2_cond_in['w1'], 'L2_cond_b1': _L2_cond_in['b1'], 'L2_cond_w2': _L2_cond_in['w2'], 'L2_cond_b2': _L2_cond_in['b2'], 'L2_cond_w_ada': _L2_cond_in['w_ada'], 'L2_cond_b_ada': _L2_cond_in['b_ada'], 'L3_cond_w_adaln': _L3_cond_in['w_adaln'], 'L3_cond_b_adaln': _L3_cond_in['b_adaln'], 'L3_cond_w_qkv': _L3_cond_in['w_qkv'], 'L3_cond_b_qkv': _L3_cond_in['b_qkv'], 'L3_cond_w_proj': _L3_cond_in['w_proj'], 'L3_cond_b_proj': _L3_cond_in['b_proj'], 'L3_cond_w_gate': _L3_cond_in['w_gate'], 'L3_cond_w1': _L3_cond_in['w1'], 'L3_cond_b1': _L3_cond_in['b1'], 'L3_cond_w2': _L3_cond_in['w2'], 'L3_cond_b2': _L3_cond_in['b2']}

def reference(x, cond_1152, L0_cond_P, L0_cond_W, L0_cond_b, L1_cond_W_qkv, L1_cond_b_qkv, L1_cond_W_proj, L1_cond_b_proj, L1_cond_W_fc1, L1_cond_b_fc1, L1_cond_W_fc2, L1_cond_b_fc2, L1_cond_W_ada, L1_cond_b_ada, L2_cond_w_qkv, L2_cond_b_qkv, L2_cond_w_proj, L2_cond_b_proj, L2_cond_qn_g, L2_cond_qn_b, L2_cond_kn_g, L2_cond_kn_b, L2_cond_w1, L2_cond_b1, L2_cond_w2, L2_cond_b2, L2_cond_w_ada, L2_cond_b_ada, L3_cond_w_adaln, L3_cond_b_adaln, L3_cond_w_qkv, L3_cond_b_qkv, L3_cond_w_proj, L3_cond_b_proj, L3_cond_w_gate, L3_cond_w1, L3_cond_b1, L3_cond_w2, L3_cond_b2):
    import jax
    import jax.numpy as jnp

    def _L0_cond_ref(x, cond, P, W, b):
        import jax, jax.numpy as jnp
        import numpy as np
        from jax.scipy.linalg import expm
        N, D, COND_DIM = (288, 64, 288)
        B, T = (16, 256)

        def _rotation(cond, W, b):
            v = jax.nn.silu(cond) @ W.T + b
            iu, ju = jnp.triu_indices(D, k=1)
            A = jnp.zeros((cond.shape[0], D, D), dtype=v.dtype)
            A = A.at[:, iu, ju].set(v).at[:, ju, iu].set(-v)
            return expm(A)
        U, _ = jnp.linalg.qr(P)
        R = _rotation(cond, W, b)
        z = jnp.einsum('btn,nd->btd', x, U)
        z_rot = jnp.einsum('btd,bde->bte', z, R)
        x_rot = x + jnp.einsum('btd,nd->btn', z_rot - z, U)
        return x_rot

    def _L1_cond_ref(x, c, W_qkv, b_qkv, W_proj, b_proj, W_fc1, b_fc1, W_fc2, b_fc2, W_ada, b_ada):
        import jax, jax.numpy as jnp
        import numpy as np
        B, L, C = (8, 256, 288)
        H = 16
        D = C // H
        FF = int(C * 4.0)
        EPS = 1e-06

        def _layernorm(x):
            mu = jnp.mean(x, axis=-1, keepdims=True)
            var = jnp.mean(jnp.square(x - mu), axis=-1, keepdims=True)
            return (x - mu) * jax.lax.rsqrt(var + EPS)

        def _modulate(x, shift, scale):
            return x * (1.0 + scale) + shift

        def _attention(h, W_qkv, b_qkv, W_proj, b_proj):
            b, l, c = h.shape
            qkv = h @ W_qkv + b_qkv
            qkv = qkv.reshape(b, l, 3, H, D)
            q, k, v = (qkv[:, :, 0], qkv[:, :, 1], qkv[:, :, 2])
            scale = D ** (-0.5)
            scores = jnp.einsum('blhd,bmhd->bhlm', q * scale, k)
            attn = jax.nn.softmax(scores, axis=-1)
            o = jnp.einsum('bhlm,bmhd->blhd', attn, v).reshape(b, l, c)
            return o @ W_proj + b_proj
        ada = jax.nn.silu(c) @ W_ada + b_ada
        shift_msa, scale_msa, gate_msa, shift_mlp, scale_mlp, gate_mlp = jnp.split(ada, 6, axis=-1)
        h = _modulate(_layernorm(x), shift_msa, scale_msa)
        x = x + gate_msa * _attention(h, W_qkv, b_qkv, W_proj, b_proj)
        h = _modulate(_layernorm(x), shift_mlp, scale_mlp)
        mlp = jax.nn.gelu(h @ W_fc1 + b_fc1, approximate=True) @ W_fc2 + b_fc2
        x = x + gate_mlp * mlp
        return x

    def _L2_cond_ref(x, c, w_qkv, b_qkv, w_proj, b_proj, qn_g, qn_b, kn_g, kn_b, w1, b1, w2, b2, w_ada, b_ada):
        import jax, jax.numpy as jnp
        import numpy as np
        HID = 288
        HEADS = 16
        HD = HID // HEADS
        MLP = int(HID * 4.0)

        def _ln(x, eps, gamma=None, beta=None):
            mu = jnp.mean(x, axis=-1, keepdims=True)
            var = jnp.mean(jnp.square(x - mu), axis=-1, keepdims=True)
            y = (x - mu) / jnp.sqrt(var + eps)
            if gamma is not None:
                y = y * gamma + beta
            return y
        B, N, C = x.shape
        H, hd = (HEADS, HD)
        scale = hd ** (-0.5)
        mod = jax.nn.silu(c) @ w_ada + b_ada
        sh_msa, sc_msa, g_msa, sh_mlp, sc_mlp, g_mlp = jnp.split(mod, 6, axis=1)
        xn = _ln(x, 1e-06)
        xn = xn * (1 + sc_msa[:, None, :]) + sh_msa[:, None, :]
        qkv = (xn @ w_qkv + b_qkv).reshape(B, N, 3, H, hd)
        q, k, v = (qkv[:, :, 0], qkv[:, :, 1], qkv[:, :, 2])
        q = _ln(q, 1e-05, qn_g, qn_b)
        k = _ln(k, 1e-05, kn_g, kn_b)
        attn = jnp.einsum('bqhd,bkhd->bhqk', q, k) * scale
        attn = jax.nn.softmax(attn, axis=-1)
        o = jnp.einsum('bhqk,bkhd->bqhd', attn, v).reshape(B, N, C)
        o = o @ w_proj + b_proj
        x = x + g_msa[:, None, :] * o
        xn2 = _ln(x, 1e-06)
        xn2 = xn2 * (1 + sc_mlp[:, None, :]) + sh_mlp[:, None, :]
        h = jax.nn.gelu(xn2 @ w1 + b1, approximate=False)
        m = h @ w2 + b2
        x = x + g_mlp[:, None, :] * m
        return x

    def _L3_cond_ref(x, c, w_adaln, b_adaln, w_qkv, b_qkv, w_proj, b_proj, w_gate, w1, b1, w2, b2):
        import jax, jax.numpy as jnp
        import numpy as np
        NUM_HEADS = 16
        NUM_EXPERTS = 4
        TOP_K = 2
        LN_EPS = 1e-06

        def _ln(h):
            mu = jnp.mean(h, axis=-1, keepdims=True)
            var = jnp.var(h, axis=-1, keepdims=True)
            return (h - mu) * jax.lax.rsqrt(var + LN_EPS)

        def _modulate(h, shift, scale):
            return h * (1.0 + scale[:, None, :]) + shift[:, None, :]
        B, N, C = x.shape
        nh = NUM_HEADS
        hd = C // nh
        mod = jax.nn.silu(c) @ w_adaln + b_adaln
        sh_msa, sc_msa, g_msa, sh_mlp, sc_mlp, g_mlp = jnp.split(mod, 6, axis=-1)
        h = _modulate(_ln(x), sh_msa, sc_msa)
        qkv = (h @ w_qkv + b_qkv).reshape(B, N, 3, nh, hd).transpose(2, 0, 3, 1, 4)
        q, k, v = (qkv[0], qkv[1], qkv[2])
        attn = jax.nn.softmax(jnp.einsum('bhqd,bhkd->bhqk', q, k) * hd ** (-0.5), axis=-1)
        o = jnp.einsum('bhqk,bhkd->bhqd', attn, v).transpose(0, 2, 1, 3).reshape(B, N, C)
        o = o @ w_proj + b_proj
        x = x + g_msa[:, None, :] * o
        xn = _modulate(_ln(x), sh_mlp, sc_mlp)
        xf = xn.reshape(-1, C)
        gate_logits = xf @ w_gate
        topk_logits, topk_idx = jax.lax.top_k(gate_logits, TOP_K)
        gates = jax.nn.softmax(topk_logits, axis=-1)
        cw = jnp.sum(jax.nn.one_hot(topk_idx, NUM_EXPERTS, dtype=xf.dtype) * gates[..., None], axis=1)
        hmid = jax.nn.gelu(jnp.einsum('tc,ech->eth', xf, w1) + b1[:, None, :], approximate=True)
        eo = jnp.einsum('eth,ehc->etc', hmid, w2) + b2[:, None, :]
        moe = jnp.einsum('te,etc->tc', cw, eo).reshape(B, N, C)
        return x + g_mlp[:, None, :] * moe
    x = _L0_cond_ref(x, cond_1152, L0_cond_P, L0_cond_W, L0_cond_b)
    x = _L1_cond_ref(x, cond_1152[:, None, :], L1_cond_W_qkv, L1_cond_b_qkv, L1_cond_W_proj, L1_cond_b_proj, L1_cond_W_fc1, L1_cond_b_fc1, L1_cond_W_fc2, L1_cond_b_fc2, L1_cond_W_ada, L1_cond_b_ada)
    x = _L2_cond_ref(x, cond_1152, L2_cond_w_qkv, L2_cond_b_qkv, L2_cond_w_proj, L2_cond_b_proj, L2_cond_qn_g, L2_cond_qn_b, L2_cond_kn_g, L2_cond_kn_b, L2_cond_w1, L2_cond_b1, L2_cond_w2, L2_cond_b2, L2_cond_w_ada, L2_cond_b_ada)
    x = _L3_cond_ref(x, cond_1152, L3_cond_w_adaln, L3_cond_b_adaln, L3_cond_w_qkv, L3_cond_b_qkv, L3_cond_w_proj, L3_cond_b_proj, L3_cond_w_gate, L3_cond_w1, L3_cond_b1, L3_cond_w2, L3_cond_b2)
    return x

_drawn_inputs = setup_inputs


def setup_inputs(seed=0):
    import zlib

    import numpy as np

    out = dict(_drawn_inputs(seed))
    spreads = {'L1_cond_b_qkv': (0.0, 0.8),
     'L1_cond_b_proj': (0.0, 0.336),
     'L1_cond_b_fc1': (0.0, 0.8),
     'L1_cond_b_fc2': (0.0, 0.355),
     'L1_cond_b_ada': (0.0, 0.372),
     'L2_cond_b_qkv': (0.0, 0.8),
     'L2_cond_b_proj': (0.0, 0.332),
     'L2_cond_qn_g': (1.0, 0.6),
     'L2_cond_qn_b': (0.0, 0.8),
     'L2_cond_kn_g': (1.0, 0.6),
     'L2_cond_kn_b': (0.0, 0.8),
     'L2_cond_b1': (0.0, 0.8),
     'L2_cond_b2': (0.0, 0.356),
     'L2_cond_b_ada': (0.0, 0.379),
     'L3_cond_b_adaln': (0.0, 0.448),
     'L3_cond_b_qkv': (0.0, 0.8),
     'L3_cond_b_proj': (0.0, 0.366),
     'L3_cond_b1': (0.0, 0.8),
     'L3_cond_b2': (0.0, 0.492)}
    factors = {'L1_cond_W_qkv': 8.0,
     'L1_cond_W_proj': 5.41,
     'L2_cond_w_qkv': 8.0,
     'L2_cond_w_proj': 5.189,
     'L3_cond_w_qkv': 8.0,
     'L3_cond_w_proj': 5.676,
     'L3_cond_w_gate': 2.859,
     'L3_cond_w1': 2.77}
    for name, (base, spread) in spreads.items():
        noise = np.random.default_rng([zlib.crc32(name.encode()), seed]).standard_normal(out[name].shape)
        drawn = base * np.exp(spread * noise) if base else spread * noise
        out[name] = jnp.asarray(drawn.astype(out[name].dtype))
    for name, factor in factors.items():
        out[name] = (out[name] * factor).astype(out[name].dtype)
    return out
```

```python
from contextlib import ExitStack

import numpy as np
import concourse.bass as bass
from concourse import mybir

F32 = mybir.dt.float32
F32R = mybir.dt.float32r
ALU = mybir.AluOpType
ACT = mybir.ActivationFunctionType
AX = mybir.AxisListType.X

B, N, C = 4, 512, 288
H, HD = 16, 18
FF = 4 * C
D = 64
LAYERS = 3
EXPERTS = (1, 1, 4)
TT = N // 128
FT = FF // 128
NM = 3
MROWS = (126, 126, 36)
SCALE = float(HD) ** -0.5
LN_EPS, QK_EPS = 1e-6, 1e-5
VW = HD + 1
ORDER = [7 * m + j for j in range(7) for m in range(NM) if 7 * m + j < H]
START = [ORDER.index(j) for j in range(7)]
WIDTH = [len([m for m in range(NM) if 7 * m + j < H]) for j in range(7)]
POSITION = [j for j in range(7) for _ in range(WIDTH[j])]
PASSES = ((0, 0), (1, 1), (0, 2), (1, 3), (2, 0), (3, 1), (4, 4))
KROWS = (128, 128, 128, 128, 96)
QR0, QR1, QR2, QROW, QK_ROWS = 0, 32, 64, 82, 82
STEPS = 4 * B
SQUARINGS, DEGREE = 14, 6
ROUNDS = DEGREE - 1 + SQUARINGS
EBASE = [sum(EXPERTS[:l]) for l in range(LAYERS + 1)]


BANK = ("ln", "q", "k", "v", "qtok", "ktok", "max", "sum", "inv", "proj")
PLAIN = (
    [(4, "q", 1, 0), (5, "q", 1, 1), (6, "q", 1, 2), (7, "k", 1, 0)],
    [(1, "k", 1, 1), (4, "k", 1, 2), (5, "proj", -1, 0), (6, "proj", -1, 1), (7, "proj", -1, 2)],
    [(1, "proj", -1, 3)] + [(4 + t, "v", 1, t) for t in range(TT)] + [(4 + t, "stats", 2, t) for t in range(TT)],
    [(0, "mean", 2, 0), (2, "scale", 2, 0), (3, "scale", 2, 1)] + [(4 + c, "ln", 2, c) for c in range(3)])
NORMED = (
    [(1, "qhat", 1, 0), (1, "ktok", 1, 0), (4, "ktok", 1, 1), (5, "ktok", 1, 2), (6, "ktok", 1, 3), (7, "q", 1, 0)],
    [(0, "khat", 1, 0), (1, "q", 1, 1), (1, "q", 1, 2), (3, "k", 1, 0), (4, "k", 1, 1), (5, "k", 1, 2),
     (6, "proj", -1, 0), (7, "proj", -1, 1)],
    [(1, "proj", -1, 2), (1, "proj", -1, 3)] + [(4 + t, "v", 1, t) for t in range(TT)] +
    [(t, "stats", 2, t) for t in range(TT)] + [(4, "mean", 2, 0), (6, "scale", 2, 0), (7, "scale", 2, 1)],
    [(1, "ln", 2, 0), (4, "ln", 2, 1), (5, "ln", 2, 2), (6, "qtok", 2, 0), (6, "qtok", 2, 1), (7, "qtok", 2, 2),
     (7, "qtok", 2, 3)])


def plan(layer, s):
    b, g = divmod(s, 4)
    out = [(0, "max", s + 1, 0)] if s + 1 < STEPS else []
    if s > 0:
        out += [(2, "sum", s - 1, 0), (3, "inv", s - 1, 0)]
    out += [(u, kind, b + d, k) for u, kind, d, k in (NORMED if layer == 1 else PLAIN)[g] if 0 <= b + d < B]
    return sorted(out, key=lambda x: x[0])


def prologue(layer):
    def norm(b):
        return [("stats", b, t) for t in range(TT)] + [("mean", b, 0)] + [("scale", b, i) for i in range(2)]

    out = norm(0) + [("ln", 0, c) for c in range(3)]
    for qk in "qk":
        if layer == 1:
            out += [(qk + "tok", 0, t) for t in range(TT)] + [(qk + "hat", 0, 0)]
        out += [(qk, 0, i) for i in range(NM)]
    out += [("v", 0, t) for t in range(TT)] + norm(1) + [("ln", 1, c) for c in range(3)]
    return out + ([("qtok", 1, t) for t in range(TT)] if layer == 1 else [])


MISC_EPILOGUE = [("sum", STEPS - 1, 0), ("inv", STEPS - 1, 0)] + [("proj", B - 1, t) for t in range(TT)]


def all_order(layer):
    seq = prologue(layer) + [("max", 0, 0)]
    for s in range(STEPS):
        seq += [x[1:] for x in plan(layer, s)]
    return seq + MISC_EPILOGUE


def misc_order(layer):
    return [key for key in all_order(layer) if key[0] in BANK]


def norm_plan(layer, b, f):
    if f == 1 and EXPERTS[layer] > 1:
        return [("gate", b, 0)]
    if f >= 6 and b + 1 < B:
        return [("ln", b + 1, f - 6)]
    return []


def norm_order(layer):
    seq = [("ln", 0, c) for c in range(3)]
    for b in range(B):
        for f_ in range(FT):
            seq += norm_plan(layer, b, f_)
    return seq


def number(orders):
    out, n = [], 0
    for seq in orders:
        out.append({key: n + i for i, key in enumerate(seq)})
        n += len(seq)
    return out


def build(nc, a, out):
    with ExitStack() as ctx:
        def sb(name, shape, dt=F32, where=ctx):
            return where.enter_context(nc.sbuf_tensor(name, shape, dt))

        ps = ctx.enter_context(nc.psum_tensor("ps", [128, 8, 512], F32))
        gate_rows = nc.dram_tensor("gate_rows", (LAYERS, B, 2, C), F32).ap()

        X = sb("X", [128, B * TT, C])
        ident = sb("ident", [128, 128])
        pick = sb("pick", [128, 4])
        ada = sb("ada", [128, LAYERS, 3, 4, B])
        stats = sb("stats", [128, TT, 6])
        mv = sb("mv", [128, TT, 2])
        var4 = sb("var4", [128, TT])
        rowt0 = sb("rowt0", [128, TT])
        rstd = sb("rstd", [128, TT])
        neghalf = sb("neghalf", [128, H])
        xn = sb("xn", [128, TT, C + 64])
        act32 = sb("act32", [128, 2, N])
        gbc = sb("gbc", [128, B, C])
        rowt = sb("rowt", [128, TT, C])

        p0 = ExitStack()
        Psb = sb("Psb", [128, 3, D], F32, p0)
        PT = sb("PT", [D, C], F32, p0)
        Wsk = sb("Wsk", [128, 3, D * (D - 1) // 2], F32, p0)
        bsk = sb("bsk", [D, D], F32, p0)
        ccol = sb("ccol", [128, 3, B], F32, p0)
        cexp = sb("cexp", [128, 3, B], F32, p0)
        csil = sb("csil", [128, 3, B], F32, p0)
        WA = sb("WA", [128, LAYERS, 3, 6 * C], F32, p0)
        bacol = sb("bacol", [128, LAYERS, 3, 4], F32, p0)
        barow = sb("barow", [B, LAYERS, 2, C], F32, p0)
        grow = sb("grow", [B, LAYERS, 2, C], F32, p0)
        T = sb("T", [D, D], F32, p0)
        GI = sb("GI", [D, 2 * D], F32, p0)
        below = sb("below", [D, D], F32, p0)
        RG = sb("RG", [D, 2, D], F32, p0)
        NB = sb("NB", [D, D], F32, p0)
        small = sb("small", [D, 2, 8], F32, p0)
        plushalf = sb("plushalf", [D, 1], F32, p0)
        RT = sb("RT", [D, D], F32, p0)
        Up = sb("Up", [D, B, D], F32, p0)
        BB = sb("BB", [D, 2, B, D], F32, p0)
        EF = sb("EF", [D, 2, 2, B, D], F32, p0)
        ident2 = sb("ident2", [D, D], F32, p0)
        XT = sb("XT", [128, 3, N], F32, p0)
        YT = sb("YT", [D, B, N], F32, p0)
        X1 = sb("X1", [D, B, D], F32, p0)
        Mid = sb("Mid", [D, B, D], F32, p0)
        YM = sb("YM", [D, 2, N], F32, p0)
        p0.close()

        pa = ExitStack()
        Q3 = sb("Q3", [96, H, N], F32R, pa)
        K3 = sb("K3", [96, H, N], F32R, pa)
        stage = sb("stage", [126, 2, 2, NM, N], F32R, pa)
        Pr = sb("Pr", [128, 2, 4, N], F32, pa)
        V = sb("V", [128, 2, TT, 320], F32, pa)
        HQ = sb("HQ", [128, 5, N], F32R, pa)
        WQ = sb("WQ", [128, 5, 3 * C], F32R, pa)
        WP = sb("WP", [128, 4, C], F32, pa)
        oT = sb("oT", [128, 5, N], F32, pa)
        rsum = sb("rsum", [128, TT, 4], F32, pa)
        ptmp = sb("ptmp", [128, C], F32, pa)
        qkcol = sb("qkcol", [126, 2, NM, 2], F32, pa)
        vrow = sb("vrow", [128, C], F32, pa)
        prow = sb("prow", [128, C], F32, pa)
        negmax = sb("negmax", [128, 2, TT, 4], F32, pa)
        mrow = sb("mrow", [4, N], F32R, pa)
        QN = sb("QN", [128, TT, C], F32, pa)
        qkrow = sb("qkrow", [128, 2, C], F32, pa)
        qstat = sb("qstat", [128, 4, TT, H], F32, pa)
        pa.close()
        RawQ = Pr[:, :, :, :].rearrange("p a h n -> p (a h n)")[:, 0:9 * C].rearrange("p (s n) -> p s n", s=3)

        pm = ExitStack()
        HM = sb("HM", [128, B, 5, N], F32R, pm)
        W1 = sb("W1", [128, 2, 5, FF], F32R, pm)
        W2 = sb("W2", [128, 2, 2, FT, C], F32R, pm)
        raw = sb("raw", [128, 2, FF], F32, pm)
        g32 = sb("g32", [128, 2, N], F32, pm)
        G = sb("G", [128, 3, 2, N], F32R, pm)
        b1col = sb("b1col", [128, 4, FT], F32, pm)
        b2row = sb("b2row", [128, 4, C], F32, pm)
        Wg = sb("Wg", [128, 5, 4], F32R, pm)
        rawg = sb("rawg", [128, 3, 4], F32, pm)
        lg = sb("lg", [128, TT, 4], F32, pm)
        wins = sb("wins", [128, TT, 6], F32, pm)
        tmp4 = sb("tmp4", [128, 2, TT, 4], F32, pm)
        chosen = sb("chosen", [128, TT, 4], F32, pm)
        top = sb("top", [128, 2, TT], F32, pm)
        cw = sb("cw", [128, B, TT, 4], F32, pm)
        pm.close()

        def sem(name):
            return ctx.enter_context(nc.semaphore(name))

        x_in = sem("x_in")
        p_in = sem("p_in")
        w_in = sem("w_in")
        ada_b_in = sem("ada_b_in")
        ada_in = [sem(f"ada_in{l}") for l in range(LAYERS)]
        consts = sem("consts")
        silu_exp = sem("silu_exp")
        silu_done = sem("silu_done")
        bc_g = sem("bc_g")
        bc_t = sem("bc_t")
        gi_upd = sem("gi_upd")
        t_upd = sem("t_upd")
        n2_ready = sem("n2_ready")
        n2_root = sem("n2_root")
        dve_done = sem("dve_done")
        pool_done = sem("pool_done")
        act_done = sem("act_done")
        skew_zero = sem("skew_zero")
        skew_mm = sem("skew_mm")
        up_ready = sem("up_ready")
        skew_t = sem("skew_t")
        skew_done = sem("skew_done")
        exp_mm = sem("exp_mm")
        exp_ev = sem("exp_ev")
        rt_ready = sem("rt_ready")
        xt_mm = sem("xt_mm")
        xt_ev = sem("xt_ev")
        y_mm = sem("y_mm")
        y_ev = sem("y_ev")
        mid_mm = sem("mid_mm")
        mid_ev = sem("mid_ev")
        ym_mm = sem("ym_mm")
        ym_ev = sem("ym_ev")
        l0_mm = sem("l0_mm")
        l0_done = sem("l0_done")
        ada_mm = sem("ada_mm")
        ada_ev = sem("ada_ev")
        gate_out = sem("gate_out")
        gram = sem("gram")
        wq_in = sem("wq_in")
        wq_split = sem("wq_split")
        wp_in = sem("wp_in")
        gate_in = sem("gate_in")
        var_ready = sem("var_ready")
        rstd_ready = sem("rstd_ready")
        xn_ready = sem("xn_ready")
        misc_full = sem("misc_full")
        misc_free = sem("misc_free")
        act_split = sem("act_split")
        a_full = sem("a_full")
        a_free = sem("a_free")
        b_full = sem("b_full")
        b_free = sem("b_free")
        av_done = sem("av_done")
        o_out = sem("o_out")
        mrow_in = sem("mrow_in")
        staged = sem("staged")
        v_ready = sem("v_ready")
        qk_var = sem("qk_var")
        qk_rstd = sem("qk_rstd")
        qn_ready = sem("qn_ready")
        att_zero = sem("att_zero")
        w_raw = [sem(f"w_raw{k}") for k in range(2)]
        w_split = sem("w_split")
        wg_in = sem("wg_in")
        wg_split = sem("wg_split")
        f_full = sem("f_full")
        f_free = sem("f_free")
        g_ready = sem("g_ready")
        g_used = sem("g_used")
        acc_full = sem("acc_full")
        acc_free = sem("acc_free")
        norm_full = sem("norm_full")
        norm_free = sem("norm_free")
        hm_ready = sem("hm_ready")
        logits = sem("logits")
        cw_exp = sem("cw_exp")
        cw_ready = sem("cw_ready")
        phase_over = sem("phase_over")
        out_done = sem("out_done")
        qk_in = [sem(f"qk_in{j}") for j in range(7)]
        MISC = number([misc_order(l) for l in range(LAYERS)])
        NORM = number([norm_order(l) for l in range(LAYERS)])
        held = []
        for l in range(LAYERS):
            held += [(l, "att", *k) for k in misc_order(l) if k[0] in ("ln", "q", "k")]
            held += [(l, "mlp", *k) for k in norm_order(l) if k[0] == "ln"]
        HELD = {k: i for i, k in enumerate(held)}

        steps = [0]

        def step():
            steps[0] += 1
            return steps[0]

        pool_steps = [0]

        def pool_step():
            pool_steps[0] += 1
            return pool_steps[0]

        def phase_begin(eng, k):
            eng.wait_ge(phase_over, 5 * k)

        def phase_end(eng):
            eng.sem_inc(phase_over, 1)

        def bc3(ap, n):
            return ap.unsqueeze(1).broadcast_to([ap.shape[0], n, ap.shape[1]])

        block = ctx.enter_context(nc.Block())

        @block.sync
        def _(sp):
            sp.dma_start(Psb[:, 0:2, :], a["P"][0:256, :].rearrange("(s p) d -> p s d", p=128)).then_inc(p_in, 16)
            sp.dma_start(Psb[0:32, 2, :], a["P"][256:C, :]).then_inc(p_in, 16)
            sp.dma_start(T[:, :], a["P"][0:D, :]).then_inc(p_in, 16)
            sp.dma_start(PT[:, :], a["PT"]).then_inc(p_in, 16)
            sp.dma_start(bsk[:, :], a["bsk"]).then_inc(p_in, 16)
            sp.dma_start(ccol[:, :, :], a["cond"]).then_inc(p_in, 16)
            for b in range(B):
                sp.dma_start(X[:, TT * b:TT * b + TT, :], a["x"][b].rearrange("(t p) c -> p t c", p=128)).then_inc(x_in, 16)
            sp.dma_start(Wsk[:, 0:2, :], a["Wsk"][0:256, :].rearrange("(s p) n -> p s n", p=128)).then_inc(w_in, 16)
            sp.dma_start(Wsk[0:32, 2, :], a["Wsk"][256:C, :]).then_inc(w_in, 16)
            sp.dma_start(bacol[:, :, :, :], a["ada_bcol"]).then_inc(ada_b_in, 16)
            for l in range(LAYERS):
                sp.dma_start(barow[:, l, :, :], a["ada_brow"][l:l + 1].broadcast_to([B, 2, C])).then_inc(ada_b_in, 16)
                sp.dma_start(WA[:, l, 0:2, :], a["ada_w"][l, 0:256, :].rearrange("(s p) n -> p s n", p=128)).then_inc(ada_in[l], 16)
                sp.dma_start(WA[0:32, l, 2, :], a["ada_w"][l, 256:C, :]).then_inc(ada_in[l], 16)
            sp.wait_ge(ada_ev, 5 * LAYERS)
            for l in range(LAYERS):
                sp.dma_start(gate_rows[l], grow[:, l, :, :]).then_inc(gate_out, 16)
            sp.wait_ge(gate_out, 16 * LAYERS)
            phase_end(sp)

            def load3(dst, src, landed):
                sp.dma_start(dst[:, 0:2, :], src[0:256, :].rearrange("(s p) n -> p s n", p=128)).then_inc(landed, 16)
                for r in range(3):
                    sp.dma_start(dst[32 * r:32 * r + 32, 2, :], src[256:C, :]).then_inc(landed, 16)

            def wide(src):
                return src.broadcast_to([128, C])

            for l in range(LAYERS):
                phase_begin(sp, 2 * l + 1)
                load3(RawQ, a["w_qkv"][l], wq_in)
                sp.dma_start(WP[:, :, :], a["w_proj"][l]).then_inc(wp_in, 16)
                sp.dma_start(qkcol[:, :, :, :], a["qkcol"][l]).then_inc(wp_in, 16)
                sp.dma_start(vrow[:, :], wide(a["vrow"][l:l + 1])).then_inc(wp_in, 16)
                sp.dma_start(prow[:, :], wide(a["prow"][l:l + 1])).then_inc(wp_in, 16)
                for i in range(2):
                    sp.dma_start(qkrow[:, i, :], wide(a["qkrow"][l, i:i + 1])).then_inc(wp_in, 16)
                for b in range(B):
                    sp.dma_start(gbc[:, b, :], wide(gate_rows[l, b, 0:1, :])).then_inc(gate_in, 16)
                sp.wait_ge(att_zero, 2 * (l + 1))

                def place(b, j):
                    if b > 0:
                        g = (START[j] + WIDTH[j] - 1) // 4
                        sp.wait_ge(b_full, 8 * (STEPS * l + 4 * (b - 1) + g + 1))
                    for qk, dst in ((0, Q3), (1, K3)):
                        for r, part in ((QR0, 0), (QR1, 1 - qk), (QR2, qk)):
                            sp.dma_start(
                                dst[r:r + HD, START[j]:START[j] + WIDTH[j], :].bitcast(F32),
                                stage[HD * j:HD * j + HD, qk, part, 0:WIDTH[j], :].bitcast(F32)).then_inc(qk_in[j], 16)

                def place_max(s):
                    sp.wait_ge(misc_free, MISC[l]["max", s, 0] + 1)
                    for i in range(4):
                        sp.dma_start(
                            Q3[QROW:QROW + 1, 4 * (s % 4) + i, :].bitcast(F32), mrow[i:i + 1, :].bitcast(F32)).then_inc(mrow_in, 16)

                sp.wait_ge(staged, 12 * (4 * l + 1))
                for j in range(7):
                    place(0, j)
                place_max(0)
                for s in range(STEPS):
                    b, g = divmod(s, 4)
                    if s + 1 < STEPS:
                        place_max(s + 1)
                    if g == 0 and b > 0:
                        place(b, 5)
                        place(b, 6)
                    if b + 1 < B:
                        if g == 1:
                            sp.wait_ge(staged, 12 * (4 * l + b + 2))
                            place(b + 1, 0)
                        if g == 2:
                            place(b + 1, 1)
                            place(b + 1, 2)
                        if g == 3:
                            place(b + 1, 3)
                            place(b + 1, 4)
                phase_end(sp)

                phase_begin(sp, 2 * l + 2)
                E = EXPERTS[l]
                sp.dma_start(b1col[:, 0:E, :], a[f"b1_{l}"]).then_inc(wg_in, 16)
                for i in range(E):
                    sp.dma_start(b2row[:, i, :], wide(a[f"b2_{l}"][i:i + 1])).then_inc(wg_in, 16)
                for b in range(B):
                    sp.dma_start(gbc[:, b, :], wide(gate_rows[l, b, 1:2, :])).then_inc(wg_in, 16)
                if E > 1:
                    load3(rawg, a["w_gate"], wg_in)
                for e in range(E):
                    for q in range(6):
                        n = 6 * (EBASE[l] + e) + q
                        if n >= 2:
                            sp.wait_ge(w_split, 2 * (n - 1))
                        if q < 2:
                            sp.dma_start(raw[:, n % 2, :], a[f"w1_{l}"][e, 128 * q:128 * q + 128, :]).then_inc(w_raw[n % 2], 16)
                        elif q == 2:
                            for r in range(3):
                                sp.dma_start(raw[32 * r:32 * r + 32, n % 2, :], a[f"w1_{l}"][e, 256:C, :]).then_inc(w_raw[n % 2], 16)
                        else:
                            k = 3 * (q - 3)
                            sp.dma_start(raw[:, n % 2, 0:3 * C].rearrange("p (t c) -> p t c", c=C),
                                 a[f"w2_{l}"][e, 128 * k:128 * (k + 3), :].rearrange("(t p) c -> p t c", p=128)).then_inc(w_raw[n % 2], 16)
                phase_end(sp)
            phase_begin(sp, 2 * LAYERS + 1)
            for b in range(B):
                sp.dma_start(out[b].rearrange("(t p) c -> p t c", p=128), X[:, TT * b:TT * b + TT, :]).then_inc(out_done, 16)
            sp.wait_ge(out_done, 16 * B)

        def wg_in_total(l):
            n = 0
            for k in range(l + 1):
                n += 1 + EXPERTS[k] + B + (4 if EXPERTS[k] > 1 else 0)
            return 16 * n

        def raw_total(n):
            return 16 * ((5, 3)[n % 2] * (n // 6) + (1, 1, 4, 2, 5, 3)[n % 6])

        @block.gpsimd
        def _(pool):
            pool.memset(ident[:, :], 0.0).then_inc(pool_done, 1)
            pool.wait_ge(pool_done, pool_step())
            pool.memset(ident2[:, :], 0.0).then_inc(pool_done, 1)
            pool.wait_ge(pool_done, pool_step())
            pool.memset(pick[:, :], 0.0).then_inc(pool_done, 1)
            pool.wait_ge(pool_done, pool_step())
            pool.memset(below[:, :], 0.0).then_inc(pool_done, 1)
            pool.wait_ge(pool_done, pool_step())
            pool.memset(neghalf[:, :], -0.5).then_inc(consts, 1)
            pool.memset(plushalf[:, :], 0.5).then_inc(consts, 1)
            pool.affine_select(out=ident[:, :], in_=ident[:, :], compare_op=ALU.not_equal, fill=1.0,
                                               base=0, pattern=[[-1, 128]], channel_multiplier=1).then_inc(consts, 1)
            pool.affine_select(out=ident2[:, :], in_=ident2[:, :], compare_op=ALU.not_equal, fill=2.0,
                                               base=0, pattern=[[-1, D]], channel_multiplier=1).then_inc(consts, 1)
            pool.affine_select(out=below[:, :], in_=below[:, :], compare_op=ALU.is_ge, fill=-1.0,
                                               base=0, pattern=[[1, D]], channel_multiplier=-1).then_inc(consts, 1)
            pool.affine_select(out=pick[:, :], in_=pick[:, :], compare_op=ALU.not_equal, fill=1.0,
                               base=-HD, pattern=[[-32, 4]], channel_multiplier=1).then_inc(consts, 1)
            pool.wait_ge(consts, 6)
            for j in range(D):
                pool.wait_ge(n2_ready, j + 1)
                pool.tensor_tensor(small[:, j % 2, 1:2], RG[:, j % 2, j:j + 1], plushalf[:, :], ALU.pow).then_inc(n2_root, 1)
            phase_end(pool)

            def norm_root(i):
                pool.wait_ge(var_ready, i + 1)
                pool.tensor_scalar(var4[:, :], mv[:, :, 1], LN_EPS, None, ALU.add).then_inc(pool_done, 1)
                pool.wait_ge(pool_done, pool_step())
                pool.tensor_tensor(rstd[:, :], var4[:, :], neghalf[:, 0:TT], ALU.pow).then_inc(rstd_ready, 1)

            def head_roots(n):
                pool.wait_ge(qk_var, n + 1)
                pool.tensor_scalar(qstat[:, 2, :, :], qstat[:, 2, :, :], 1.0 / HD, QK_EPS, ALU.mult, ALU.add).then_inc(pool_done, 1)
                pool.wait_ge(pool_done, pool_step())
                pool.tensor_tensor(qstat[:, 3, :, :], qstat[:, 2, :, :], bc3(neghalf[:, :], TT), ALU.pow).then_inc(qk_rstd, 1)

            for l in range(LAYERS):
                phase_begin(pool, 2 * l + 1)
                pool.memset(K3[0:64, :, :].bitcast(F32), 0.0).then_inc(pool_done, 1)
                pool.wait_ge(pool_done, pool_step())
                pool.memset(K3[64:96, :, :].bitcast(F32), 1.0).then_inc(pool_done, 1)
                pool.wait_ge(pool_done, pool_step())
                pool.memset(V[:, :, :, :], 1.0).then_inc(att_zero, 1)
                for kind, b, k in all_order(l):
                    if kind == "mean":
                        norm_root(8 * l + b)
                    if kind in ("qtok", "ktok") and k == TT - 1:
                        head_roots(2 * b + "qk".index(kind[0]))
                phase_end(pool)
                phase_begin(pool, 2 * l + 2)
                for b in range(B):
                    norm_root(8 * l + 4 + b)
                phase_end(pool)

        @block.vector
        def _(dve):
            dve.memset(ps[0:D, 6, 0:B * D], 0.0).then_inc(skew_zero, 1)
            dve.wait_ge(p_in, 96)
            dve.wait_ge(consts, 6)
            dve.wait_ge(silu_exp, 1)
            dve.tensor_scalar(cexp[:, :, :], cexp[:, :, :], 1.0, None, ALU.add).then_inc(dve_done, 1)
            dve.wait_ge(dve_done, step())
            dve.reciprocal(cexp[:, :, :], cexp[:, :, :]).then_inc(dve_done, 1)
            dve.wait_ge(dve_done, step())
            dve.tensor_tensor(csil[:, :, :], ccol[:, :, :], cexp[:, :, :], ALU.mult).then_inc(silu_done, 1)
            dve.tensor_copy(GI[:, D:2 * D], ident[0:D, 0:D])
            dve.wait_ge(gram, 1)
            dve.tensor_copy(GI[:, 0:D], ps[0:D, 0, 0:D]).then_inc(gi_upd, 1)
            dve.wait_ge(gi_upd, 1)

            def reduce_gram(j):
                k, r, m = j % 2, small[:, j % 2, 0:1], small[:, j % 2, 2:3]
                row = ps[0:D, k, 0:2 * D]
                dve.wait_ge(bc_g, j + 1)
                dve.reciprocal(r, row[:, j:j + 1]).then_inc(dve_done, 1)
                dve.wait_ge(dve_done, step())
                dve.scalar_tensor_tensor(out=m, in0=GI[:, j:j + 1], scalar=r, in1=below[:, j:j + 1],
                                               op0=ALU.mult, op1=ALU.mult).then_inc(dve_done, 1)
                dve.wait_ge(dve_done, step())
                dve.scalar_tensor_tensor(out=GI[:, :], in0=row, scalar=m, in1=GI[:, :],
                                                         op0=ALU.mult, op1=ALU.add).then_inc(gi_upd, 1)
                dve.tensor_copy(RG[:, k, :], row[:, 0:D]).then_inc(n2_ready, 1)

            def reduce_top(j):
                k = j % 2
                n2, root = RG[:, k, j:j + 1], small[:, k, 1:2]
                sg, den, rd, m, nb = small[:, k, 3:4], small[:, k, 4:5], small[:, k, 5:6], small[:, k, 6:7], NB[:, j:j + 1]
                row = ps[0:D, 2 + k, 0:D]
                alpha = row[:, j:j + 1]
                dve.wait_ge(bc_t, j + 1)
                dve.tensor_scalar(sg, alpha, 0.0, 2.0, ALU.is_ge, ALU.mult).then_inc(dve_done, 1)
                dve.wait_ge(dve_done, step())
                dve.wait_ge(n2_root, j + 1)
                dve.wait_ge(n2_ready, j + 1)
                dve.tensor_scalar(nb, sg, -1.0, root, ALU.add, ALU.mult).then_inc(dve_done, 1)
                dve.wait_ge(dve_done, step())
                dve.tensor_scalar(den, alpha, nb, n2, ALU.mult, ALU.add).then_inc(dve_done, 1)
                dve.wait_ge(dve_done, step())
                dve.reciprocal(rd, den).then_inc(dve_done, 1)
                dve.wait_ge(dve_done, step())
                dve.scalar_tensor_tensor(out=m, in0=T[:, j:j + 1], scalar=rd, in1=below[:, j:j + 1],
                                         op0=ALU.mult, op1=ALU.mult)
                dve.scalar_tensor_tensor(out=RG[:, k, :], in0=row, scalar=nb, in1=RG[:, k, :],
                                               op0=ALU.mult, op1=ALU.add).then_inc(dve_done, 1)
                dve.wait_ge(dve_done, step())
                dve.scalar_tensor_tensor(out=T[:, :], in0=RG[:, k, :], scalar=m, in1=T[:, :],
                                                        op0=ALU.mult, op1=ALU.add).then_inc(t_upd, 1)

            def skew_add():
                dve.wait_ge(skew_mm, 1)
                dve.tensor_tensor(Up[:, :, :], ps[0:D, 6, 0:B * D].rearrange("p (b j) -> p b j", b=B),
                                                    bc3(bsk[:, :], B), ALU.add).then_inc(up_ready, 1)

            def skew_scale():
                dve.wait_ge(skew_t, 1)
                dve.wait_ge(up_ready, 1)
                dve.scalar_tensor_tensor(out=Up[:, :, :], in0=ps[0:D, 7, 0:B * D].rearrange("p (b j) -> p b j", b=B),
                                               scalar=-1.0, in1=Up[:, :, :], op0=ALU.mult, op1=ALU.add).then_inc(dve_done, 1)
                dve.wait_ge(dve_done, step())
                sc = 2.0 ** -SQUARINGS
                for i, x in enumerate((sc, -sc)):
                    dve.tensor_scalar(BB[:, i, :, :], Up[:, :, :], x, None, ALU.mult).then_inc(skew_done, 1)
                    dve.tensor_scalar(EF[:, 0, i, :, :], Up[:, :, :], x / DEGREE, None, ALU.mult).then_inc(skew_done, 1)

            def ada_add(l):
                dve.wait_ge(ada_mm, l + 1)
                dve.wait_ge(ada_b_in, 16 * (1 + LAYERS))
                n = 8 * B
                for rows, lo, hi in ((128, 0, 2), (96, 2, 3)):
                    dve.tensor_tensor(
                        ada[0:rows, l, lo:hi, :, :].rearrange("p c v b -> p (c v) b"),
                        ps[0:rows, 4, 4 * B * lo:4 * B * hi].rearrange("p (x b) -> p x b", b=B),
                        bacol[0:rows, l, lo:hi, :].rearrange("p c v -> p (c v)").unsqueeze(2).broadcast_to(
                            [rows, 4 * (hi - lo), B]), ALU.add).then_inc(ada_ev, 1)
                dve.wait_ge(ada_ev, 5 * l + 2)
                for rows, lo, hi in ((128, 0, 2), (96, 2, 3)):
                    for c in range(lo, hi):
                        x = ada[0:rows, l, c, 1::2, :]
                        ins = dve.tensor_scalar(x, x, 1.0, None, ALU.add)
                ins.then_inc(ada_ev, 1)
                for i, bank in ((0, 5), (1, 7)):
                    dve.tensor_tensor(grow[:, l, i, :], ps[0:B, bank, 0:C], barow[:, l, i, :], ALU.add).then_inc(ada_ev, 1)

            for j in range(D):
                reduce_gram(j)
                if j > 0:
                    reduce_top(j - 1)
                if j == 28:
                    skew_add()
                if j == 29:
                    skew_scale()
                if j in ADA_AT:
                    ada_add(ADA_AT.index(j))
            reduce_top(D - 1)
            dve.wait_ge(t_upd, D)
            dve.wait_ge(gi_upd, D + 1)
            dve.tensor_tensor(NB[:, :], NB[:, :], ident[0:D, 0:D], ALU.mult).then_inc(dve_done, 1)
            dve.wait_ge(dve_done, step())
            dve.tensor_reduce(small[:, 0, 0:1], NB[:, :], AX, ALU.add, negate=True).then_inc(dve_done, 1)
            dve.wait_ge(dve_done, step())
            dve.reciprocal(small[:, 0, 1:2], small[:, 0, 0:1]).then_inc(dve_done, 1)
            dve.wait_ge(dve_done, step())
            dve.tensor_scalar(RT[:, :], GI[:, D:2 * D], small[:, 0, 1:2], None, ALU.mult).then_inc(rt_ready, 1)
            for b in range(B):
                for t in range(TT):
                    n = TT * b + t
                    dve.wait_ge(l0_mm, n + 1)
                    dve.tensor_tensor(X[:, n, :], X[:, n, :], ps[:, 4 + t, 0:C], ALU.add).then_inc(l0_done, 1)
            phase_end(dve)

            def norm_stats(b, t):
                dve.bn_stats(stats[:, t, :], X[:, TT * b + t, :]).then_inc(dve_done, 1)
                step()

            def norm_mean():
                dve.wait_ge(dve_done, steps[0])
                for t in range(TT):
                    dve.bn_aggr(mv[:, t, :], stats[:, t, :]).then_inc(dve_done, 1)
                    step()
                dve.wait_ge(dve_done, steps[0])
                dve.tensor_copy(rowt0[:, 0:TT], mv[:, :, 0]).then_inc(var_ready, 1)

            def norm_scale(i, b, tiles):
                dve.wait_ge(rstd_ready, i + 1)
                for t in tiles:
                    dve.tensor_scalar(xn[:, t, 0:C], X[:, TT * b + t, :], mv[:, t, 0:1], rstd[:, t:t + 1],
                                      ALU.subtract, ALU.mult).then_inc(dve_done, 1)
                    step()
                dve.wait_ge(dve_done, steps[0])
                for r in range(2):
                    dve.tensor_copy(xn[:, tiles[0]:tiles[-1] + 1, C + 32 * r:C + 32 * r + 32],
                                    xn[:, tiles[0]:tiles[-1] + 1, C - 32:C]).then_inc(xn_ready, 1)

            def norm(i, b, free):
                for t in range(TT):
                    norm_stats(b, t)
                norm_mean()
                free()
                norm_scale(i, b, (0, 1))
                norm_scale(i, b, (2, 3))

            def split_tokens(src, dst, c):
                if c < 2:
                    dve.tensor_copy(dst[:, c, :], src[:, :]).then_inc(dve_done, 1)
                    dve.wait_ge(dve_done, step())
                    return dve.tensor_tensor(dst[:, 2 + c, :], src[:, :], dst[:, c, :].bitcast(F32), ALU.subtract)
                dve.tensor_copy(dst[0:96, 4, :], src[0:96, :]).then_inc(dve_done, 1)
                dve.wait_ge(dve_done, step())
                return dve.tensor_tensor(dst[32:64, 4, :], src[32:64, :], dst[32:64, 4, :].bitcast(F32), ALU.subtract)

            def split_weights(dst, src, c):
                if c < 2:
                    dve.tensor_copy(dst[:, c, :], src[:, :]).then_inc(dve_done, 1)
                    dve.wait_ge(dve_done, step())
                    return dve.tensor_tensor(dst[:, 2 + c, :], src[:, :], dst[:, c, :].bitcast(F32), ALU.subtract)
                dve.tensor_copy(dst[0:96, 4, :], src[0:96, :]).then_inc(dve_done, 1)
                dve.wait_ge(dve_done, step())
                return dve.tensor_tensor(dst[64:96, 4, :], src[64:96, :], dst[64:96, 4, :].bitcast(F32), ALU.subtract)

            for l in range(LAYERS):
                M, W = MISC[l], NORM[l]
                phase_begin(dve, 2 * l + 1)
                dve.memset(Q3[:, :, :].bitcast(F32), 0.0).then_inc(att_zero, 1)


                def heads_of(qk):
                    return rowt[:, :, :] if qk else QN[:, :, :]

                def work(kind, i, k):
                    if kind == "max":
                        return
                    if kind == "stats":
                        norm_stats(i, k)
                        return
                    if kind == "mean":
                        norm_mean()
                        return
                    if kind == "scale":
                        if i > 0 and k == 0:
                            dve.wait_ge(misc_full, M["ln", i - 1, 2] + 1)
                        norm_scale(8 * l + i, i, (2 * k, 2 * k + 1))
                        return
                    if kind in ("qhat", "khat"):
                        qk = "qk".index(kind[0])
                        dve.wait_ge(qk_rstd, 2 * i + qk + 1)
                        x = heads_of(qk).rearrange("p t (h e) -> p (t h) e", e=HD)
                        r = qstat[:, 3, :, :].rearrange("p t h -> p (t h)").unsqueeze(2).broadcast_to([128, TT * H, HD])
                        dve.tensor_tensor(x, x, r, ALU.mult).then_inc(qn_ready, 1)
                        return
                    n = M[kind, i, k]
                    if kind in ("ln", "q", "k"):
                        h = HELD[l, "att", kind, i, k]
                        src = act32[:, h % 2, :]
                        if kind == "ln" and k == 0 and i > 0:
                            dve.wait_ge(misc_full, M["v", i - 1, TT - 1] + 1)
                        if kind == "q" and k == 0 and i > 0:
                            for placed in qk_in:
                                dve.wait_ge(placed, 96 * (4 * l + i))
                        dve.wait_ge(misc_free, n + 1)
                        if kind == "ln":
                            split_tokens(src, HQ, k).then_inc(act_split, 1)
                            return
                        rows, qk = MROWS[k], "qk".index(kind)
                        dve.tensor_copy(stage[0:rows, qk, 0, k, :], src[0:rows, :]).then_inc(staged, 1)
                        dve.wait_ge(staged, 12 * (4 * l + i) + 6 * qk + 2 * k + 1)
                        dve.tensor_tensor(stage[0:rows, qk, 1, k, :], src[0:rows, :],
                                                          stage[0:rows, qk, 0, k, :].bitcast(F32), ALU.subtract).then_inc(staged, 1)
                        return
                    dve.wait_ge(misc_full, n + 1)
                    bank = ps[:, 7, :]
                    if kind == "v":
                        if k == 0:
                            if i == 0:
                                dve.wait_ge(att_zero, 2 * (l + 1))
                            if i >= 2:
                                dve.wait_ge(av_done, 4 * (STEPS * l + 4 * (i - 1)))
                        dve.tensor_tensor(
                            V[:, i % 2, k, 0:H * VW].rearrange("p (h e) -> p h e", e=VW)[:, :, 0:HD],
                            bank[:, 0:C].rearrange("p (h e) -> p h e", e=HD),
                            vrow[:, :].rearrange("p (h e) -> p h e", e=HD), ALU.add).then_inc(misc_free, 1)
                    elif kind == "sum":
                        dve.reciprocal(rsum[:, :, :], bank[:, 0:4 * TT].rearrange("p (t j) -> p t j", j=4)).then_inc(misc_free, 1)
                    elif kind == "inv":
                        dve.wait_ge(o_out, STEPS * l + i + 1)
                        dve.tensor_tensor(oT[:, i % 5, :], oT[:, i % 5, :], bank, ALU.mult).then_inc(misc_free, 1)
                    elif kind == "proj":
                        x = ptmp[:, :]
                        dve.wait_ge(dve_done, steps[0])
                        dve.tensor_tensor(x, bank[:, 0:C], prow[:, :], ALU.add).then_inc(misc_free, 1)
                        dve.wait_ge(misc_free, n + 1)
                        dve.tensor_tensor(x, x, gbc[:, i, :], ALU.mult).then_inc(dve_done, 1)
                        dve.wait_ge(dve_done, step())
                        dve.tensor_tensor(X[:, TT * i + k, :], X[:, TT * i + k, :], x, ALU.add).then_inc(dve_done, 1)
                        step()
                    elif kind in ("qtok", "ktok"):
                        qk = "qk".index(kind[0])
                        t, sq = heads_of(qk)[:, k, :], ptmp[:, :]
                        th, sh = (x.rearrange("p (h e) -> p h e", e=HD) for x in (t, sq))
                        if k == 0 and i > 0:
                            dve.wait_ge(misc_full, M["qk"[qk], i - 1, NM - 1] + 1)
                        dve.tensor_tensor(t, bank[:, 0:C], qkrow[:, qk, :], ALU.add).then_inc(misc_free, 1)
                        dve.wait_ge(misc_free, n + 1)
                        if k == 0 and 2 * i + qk > 0:
                            dve.wait_ge(qn_ready, 2 * i + qk)
                        dve.tensor_reduce(qstat[:, 0, k, :], th, AX, ALU.add).then_inc(dve_done, 1)
                        dve.wait_ge(dve_done, step())
                        dve.tensor_scalar(qstat[:, 1, k, :], qstat[:, 0, k, :], 1.0 / HD, None, ALU.mult).then_inc(dve_done, 1)
                        dve.wait_ge(dve_done, step())
                        dve.tensor_tensor(th, th, qstat[:, 1, k, :].unsqueeze(2).broadcast_to([128, H, HD]),
                                          ALU.subtract).then_inc(dve_done, 1)
                        dve.wait_ge(dve_done, step())
                        dve.tensor_tensor(sq, t, t, ALU.mult).then_inc(dve_done, 1)
                        dve.wait_ge(dve_done, step())
                        dve.tensor_reduce(qstat[:, 2, k, :], sh, AX, ALU.add).then_inc(dve_done if k < TT - 1 else qk_var, 1)
                        if k < TT - 1:
                            dve.wait_ge(dve_done, step())
                        else:
                            dve.wait_ge(qk_var, 2 * i + qk + 1)

                def negmax_unit(s, i):
                    n = 16 * (STEPS * l + s) + i
                    if i == 0 and s >= 2:
                        dve.wait_ge(misc_full, M["max", s - 2, 0] + 1)
                    dve.wait_ge(a_full, n + 1)
                    dve.tensor_reduce(negmax[:, s % 2, i % 4, i // 4:i // 4 + 1], ps[:, 4 + i % 2, :],
                                                      AX, ALU.max, negate=True).then_inc(a_free, 1)

                for key in prologue(l):
                    work(*key)
                    if key == ("scale", 0, 1):
                        dve.wait_ge(wq_in, 64 * (l + 1))
                        for c in range(3):
                            split_weights(WQ, RawQ[:, c, :], c).then_inc(wq_split, 1)
                        dve.wait_ge(wp_in, 96 * (l + 1))
                        dve.wait_ge(gate_in, 16 * B * (l + 1))
                for s in range(2):
                    for i in range(16):
                        negmax_unit(s, i)
                for s in range(STEPS):
                    for u in range(8):
                        for at, *key in plan(l, s):
                            if at == u:
                                work(*key)
                        if s + 2 < STEPS:
                            negmax_unit(s + 2, 2 * u)
                            negmax_unit(s + 2, 2 * u + 1)
                for key in MISC_EPILOGUE:
                    work(*key)
                dve.wait_ge(dve_done, steps[0])
                phase_end(dve)

                phase_begin(dve, 2 * l + 2)
                E = EXPERTS[l]

                def mlp_norm(b):
                    def free():
                        dve.wait_ge((norm_full if b else misc_full), (W["ln", b - 1, 2] if b else M["ln", B - 1, 2]) + 1)
                    norm(8 * l + 4 + b, b, free)

                def mlp_split(b, c):
                    h = HELD[l, "mlp", "ln", b, c]
                    dve.wait_ge(norm_free, W["ln", b, c] + 1)
                    split_tokens(act32[:, h % 2, :], HM[:, b], c).then_inc(hm_ready, 1)

                def piece(e, q):
                    n = 6 * (EBASE[l] + e) + q
                    k = (EBASE[l] + e) % 2
                    dve.wait_ge(w_raw[n % 2], raw_total(n))
                    src = raw[:, n % 2, :]
                    if e > 0:
                        dve.wait_ge(acc_full, 4 * B * (EBASE[l] + e - 1)) if e > 1 or l > 0 else None
                    if q < 3:
                        if q < 2:
                            hi, lo, s_ = W1[:, k, q, :], W1[:, k, 2 + q, :], src
                            dve.tensor_copy(hi, s_).then_inc(w_split, 1)
                            dve.wait_ge(w_split, 2 * n + 1)
                            dve.tensor_tensor(lo, s_, hi.bitcast(F32), ALU.subtract).then_inc(w_split, 1)
                        else:
                            dve.tensor_copy(W1[0:96, k, 4, :], src[0:96, :]).then_inc(w_split, 1)
                            dve.wait_ge(w_split, 2 * n + 1)
                            dve.tensor_tensor(W1[64:96, k, 4, :], src[64:96, :],
                                                               W1[64:96, k, 4, :].bitcast(F32), ALU.subtract).then_inc(w_split, 1)
                    else:
                        j = 3 * (q - 3)
                        s_ = src[:, 0:3 * C].rearrange("p (t c) -> p t c", c=C)
                        dve.tensor_copy(W2[:, k, 0, j:j + 3, :], s_).then_inc(w_split, 1)
                        dve.wait_ge(w_split, 2 * n + 1)
                        dve.tensor_tensor(W2[:, k, 1, j:j + 3, :], s_,
                                                           W2[:, k, 0, j:j + 3, :].bitcast(F32), ALU.subtract).then_inc(w_split, 1)

                def split_hidden(n):
                    dve.wait_ge(f_free, n + 1)
                    if n >= 3:
                        U, ft = divmod(n - 3, FT)
                        if ft < FT - 1:
                            dve.wait_ge(g_used, (FT - 1) * U + ft + 1)
                        else:
                            dve.wait_ge(acc_full, TT * (U + 1))
                    x, k = g32[:, n % 2, :], n % 3
                    dve.tensor_copy(G[:, k, 0, :], x).then_inc(g_ready, 1)
                    dve.wait_ge(g_ready, 2 * n + 1)
                    dve.tensor_tensor(G[:, k, 1, :], x, G[:, k, 0, :].bitcast(F32), ALU.subtract).then_inc(g_ready, 1)

                def finish(U, e, b):
                    for t in range(TT):
                        dve.wait_ge(acc_full, TT * U + t + 1)
                        dve.tensor_tensor(rowt[:, t, :], ps[:, t, 0:C], b2row[:, e, :], ALU.add).then_inc(acc_free, 1)
                    dve.wait_ge(acc_free, TT * (U + 1))
                    dve.tensor_tensor(rowt[:, :, :], rowt[:, :, :], bc3(gbc[:, b, :], TT), ALU.mult).then_inc(dve_done, 1)
                    dve.wait_ge(dve_done, step())
                    xs = X[:, TT * b:TT * b + TT, :]
                    if E == 1:
                        dve.tensor_tensor(xs, xs, rowt[:, :, :], ALU.add).then_inc(dve_done, 1)
                        dve.wait_ge(dve_done, step())
                    else:
                        for t in range(TT):
                            dve.scalar_tensor_tensor(out=X[:, TT * b + t, :], in0=rowt[:, t, :],
                                                                  scalar=cw[:, b, t, e:e + 1], in1=X[:, TT * b + t, :],
                                                                  op0=ALU.mult, op1=ALU.add).then_inc(dve_done, 1)
                            step()
                        dve.wait_ge(dve_done, steps[0])

                def choose(b):
                    dve.wait_ge(norm_full, W["gate", b, 0] + 1)
                    dve.tensor_copy(lg[:, :, :], ps[:, 7, 0:4 * TT].rearrange("p (t e) -> p t e", e=4)).then_inc(norm_free, 1)
                    dve.wait_ge(norm_free, W["gate", b, 0] + 1)
                    dve.tensor_reduce(top[:, 0, :], lg[:, :, :], AX, ALU.max).then_inc(dve_done, 1)
                    dve.wait_ge(dve_done, step())
                    dve.tensor_tensor(tmp4[:, 0, :, :], lg[:, :, :],
                                                      top[:, 0, :].unsqueeze(2).broadcast_to([128, TT, 4]), ALU.subtract).then_inc(logits, 1)
                    pairs = ((0, 1), (0, 2), (0, 3), (1, 2), (1, 3), (2, 3))
                    for p, (i, j) in enumerate(pairs):
                        dve.tensor_tensor(wins[:, :, p:p + 1], lg[:, :, i:i + 1], lg[:, :, j:j + 1], ALU.is_ge).then_inc(dve_done, 1)
                        step()
                    dve.wait_ge(dve_done, steps[0])

                    def w(i, j):
                        p = pairs.index((i, j))
                        return wins[:, :, p:p + 1]

                    c = [chosen[:, :, e:e + 1] for e in range(4)]
                    dve.tensor_tensor(c[0], w(0, 1), w(0, 2), ALU.add).then_inc(dve_done, 1)
                    step()
                    dve.tensor_tensor(c[1], w(0, 1), w(1, 2), ALU.subtract).then_inc(dve_done, 1)
                    step()
                    dve.tensor_tensor(c[2], w(0, 2), w(1, 2), ALU.add).then_inc(dve_done, 1)
                    step()
                    dve.tensor_tensor(c[3], w(0, 3), w(1, 3), ALU.add).then_inc(dve_done, 1)
                    step()
                    dve.wait_ge(dve_done, steps[0])
                    dve.tensor_tensor(c[0], c[0], w(0, 3), ALU.add).then_inc(dve_done, 1)
                    step()
                    dve.tensor_tensor(c[1], c[1], w(1, 3), ALU.subtract).then_inc(dve_done, 1)
                    step()
                    dve.tensor_tensor(c[2], c[2], w(2, 3), ALU.subtract).then_inc(dve_done, 1)
                    step()
                    dve.tensor_tensor(c[3], c[3], w(2, 3), ALU.add).then_inc(dve_done, 1)
                    step()
                    dve.wait_ge(dve_done, steps[0])
                    for e, (op, x) in enumerate(((ALU.is_ge, 2.0), (ALU.is_lt, 0.0), (ALU.is_lt, 1.0), (ALU.is_lt, 2.0))):
                        dve.tensor_scalar(c[e], c[e], x, None, op).then_inc(dve_done, 1)
                        step()
                    dve.wait_ge(dve_done, steps[0])

                def weigh(b):
                    dve.wait_ge(cw_exp, b + 1)
                    dve.tensor_tensor(tmp4[:, 1, :, :], tmp4[:, 1, :, :], chosen[:, :, :], ALU.mult).then_inc(dve_done, 1)
                    dve.wait_ge(dve_done, step())
                    dve.tensor_reduce(top[:, 0, :], tmp4[:, 1, :, :], AX, ALU.add).then_inc(dve_done, 1)
                    dve.wait_ge(dve_done, step())
                    dve.reciprocal(top[:, 1, :], top[:, 0, :]).then_inc(dve_done, 1)
                    dve.wait_ge(dve_done, step())
                    dve.tensor_tensor(cw[:, b, :, :], tmp4[:, 1, :, :],
                                            top[:, 1, :].unsqueeze(2).broadcast_to([128, TT, 4]), ALU.mult).then_inc(dve_done, 1)
                    dve.wait_ge(dve_done, step())

                mlp_norm(0)
                for q in range(3):
                    piece(0, q)
                for c in range(3):
                    mlp_split(0, c)
                for q in range(3, 6):
                    piece(0, q)
                dve.wait_ge(wg_in, wg_in_total(l))
                if E > 1:
                    for c in range(3):
                        split_weights(Wg, rawg[:, c, :], c).then_inc(wg_split, 1)
                units = [(e, b) for e in range(E) for b in range(B)]
                for v, (e, b) in enumerate(units):
                    U = B * EBASE[l] + v
                    for ft in range(FT):
                        if e == 0:
                            if ft == 4 and b + 1 < B:
                                mlp_norm(b + 1)
                            for kind, i, c in norm_plan(l, b, ft):
                                if kind == "gate":
                                    choose(i)
                                else:
                                    mlp_split(i, c)
                            if E > 1 and ft == 3:
                                weigh(b)
                        split_hidden(FT * U + ft)
                        if ft == 1 and v > 0:
                            finish(U - 1, *units[v - 1])
                        if e + 1 < E and b > 0 and ft in (3, 6):
                            piece(e + 1, 2 * (b - 1) + (ft == 6))
                finish(B * EBASE[l] + len(units) - 1, *units[-1])
                phase_end(dve)

        @block.scalar
        def _(act):
            act.wait_ge(p_in, 96)
            act.activation(cexp[:, :, :], ccol[:, :, :], ACT.Exp, scale=-1.0).then_inc(silu_exp, 1)

            def xt_copy(b, c):
                n = 3 * b + c
                rows = 128 if c < 2 else 32
                act.wait_ge(xt_mm, n + 1)
                if b > 0:
                    act.wait_ge(y_mm, b)
                act.activation(XT[0:rows, c, :], ps[0:rows, 4, :], ACT.Copy).then_inc(xt_ev, 1)

            def y_copy(b):
                act.wait_ge(y_mm, b + 1)
                act.activation(YT[:, b, :], ps[0:D, 5, :], ACT.Copy).then_inc(y_ev, 1)

            def exp_copy(r):
                act.wait_ge(exp_mm, 2 * r + 2)
                k = 1.0 / (DEGREE - 1 - r) if r < DEGREE - 1 else 1.0
                act.activation(EF[:, (r + 1) % 2].rearrange("p x b j -> p (x b j)"), ps[0:D, 6, :],
                                               ACT.Copy, scale=k).then_inc(exp_ev, 1)

            for b in range(B):
                for c in range(3):
                    xt_copy(b, c)
                y_copy(b)
            for r in range(ROUNDS):
                exp_copy(r)
            act.wait_ge(mid_mm, 1)
            act.activation(X1[:, :, :].rearrange("p b j -> p (b j)"), ps[0:D, 0, 0:B * D], ACT.Copy).then_inc(mid_ev, 1)
            act.wait_ge(mid_mm, 2)
            act.activation(Mid[:, :, :].rearrange("p b j -> p (b j)"), ps[0:D, 1, 0:B * D], ACT.Copy).then_inc(mid_ev, 1)
            for b in range(B):
                act.wait_ge(ym_mm, b + 1)
                if b >= 2:
                    act.wait_ge(l0_mm, TT * (b - 1))
                act.activation(YM[:, b % 2, :], ps[0:D, 2 + b % 2, :], ACT.Copy).then_inc(ym_ev, 1)
            phase_end(act)

            def hold(where, l, key):
                h = HELD[(l, where, *key)]
                if h >= 2:
                    pl, pw, *pk = held[h - 2]
                    if pw == "mlp":
                        act.wait_ge(hm_ready, 3 * (4 * pl + pk[1]) + pk[2] + 1)
                    elif pk[0] == "ln":
                        act.wait_ge(act_split, 3 * (4 * pl + pk[1]) + pk[2] + 1)
                    else:
                        act.wait_ge(staged, 12 * (4 * pl + pk[1]) + 6 * "qk".index(pk[0]) + 2 * pk[2] + 2)
                return act32[:, h % 2, :]

            for l in range(LAYERS):
                M, W = MISC[l], NORM[l]
                phase_begin(act, 2 * l + 1)
                act.wait_ge(wp_in, 96 * (l + 1))

                def work(kind, i, k):
                    n = M[kind, i, k]
                    if kind == "max":
                        act.wait_ge(misc_full, n + 1)
                        if STEPS * l + i > 0:
                            act.wait_ge(mrow_in, 64 * (STEPS * l + i))
                        act.activation(mrow[:, :], ps[0:4, 7, :], ACT.Copy).then_inc(misc_free, 1)
                    elif kind == "ln":
                        act.wait_ge(misc_full, n + 1)
                        rows = 128 if k < 2 else 96
                        dst = hold("att", l, (kind, i, k))
                        act.activation(dst[0:rows, :], ps[0:rows, 7, :], ACT.Identity,
                                                          bias=ada[0:rows, l, k, 0, i:i + 1],
                                                          scale=ada[0:rows, l, k, 1, i:i + 1]).then_inc(misc_free, 1)
                    elif kind in ("q", "k"):
                        act.wait_ge(misc_full, n + 1)
                        rows, qk = MROWS[k], "qk".index(kind)
                        dst = hold("att", l, (kind, i, k))
                        act.activation(dst[0:rows, :], ps[0:rows, 7, :], ACT.Identity,
                                                          bias=qkcol[0:rows, qk, k, 1:2],
                                                          scale=qkcol[0:rows, qk, k, 0:1] if l == 1 else 1.0).then_inc(misc_free, 1)

                def exp_unit(s, u):
                    n, v = 8 * (STEPS * l + s) + u, 4 * (STEPS * l + s) + u // 2
                    if n == 8 * STEPS * l:
                        act.wait_ge(wq_split, 3 * (l + 1))
                    act.wait_ge(b_full, n + 1)
                    if v >= 2:
                        act.wait_ge(av_done, v - 1)
                    act.activation(Pr[:, (u // 2) % 2, 2 * (u % 2):2 * (u % 2) + 2, :],
                                                   ps[:, 2 * (u % 2):2 * (u % 2) + 2, :], ACT.Exp, scale=SCALE).then_inc(b_free, 1)

                def take_o(s):
                    n = STEPS * l + s
                    act.wait_ge(av_done, 4 * (n + 1))
                    if s >= 5:
                        act.wait_ge(misc_full, M["proj", (s - 5) // 4, TT - 1] + 1)
                    act.activation(oT[:, s % 5, :], ps[:, 6, :], ACT.Copy).then_inc(o_out, 1)

                for key in prologue(l) + [("max", 0, 0)]:
                    if key[0] in BANK:
                        work(*key)
                for s in range(STEPS):
                    for u in range(8):
                        for at, *key in plan(l, s):
                            if at == u and key[0] in BANK:
                                work(*key)
                        exp_unit(s, u)
                        if u == 1 and s > 0:
                            take_o(s - 1)
                take_o(STEPS - 1)
                phase_end(act)

                phase_begin(act, 2 * l + 2)
                act.wait_ge(wg_in, wg_in_total(l))
                E = EXPERTS[l]
                gelu = ACT.Gelu if l == 1 else ACT.Gelu_apprx_tanh

                def take_norm(b, c):
                    rows = 128 if c < 2 else 96
                    act.wait_ge(norm_full, W["ln", b, c] + 1)
                    dst = hold("mlp", l, ("ln", b, c))
                    act.activation(dst[0:rows, :], ps[0:rows, 7, :], ACT.Identity,
                                                      bias=ada[0:rows, l, c, 2, b:b + 1],
                                                      scale=ada[0:rows, l, c, 3, b:b + 1]).then_inc(norm_free, 1)

                for c in range(3):
                    take_norm(0, c)
                for v in range(E * B):
                    e, b = divmod(v, B)
                    for ft in range(FT):
                        n = FT * (B * EBASE[l] + v) + ft
                        if e == 0:
                            for kind, i, c in norm_plan(l, b, ft):
                                if kind == "ln":
                                    take_norm(i, c)
                            if E > 1 and ft == 2:
                                act.wait_ge(logits, b + 1)
                                act.activation(tmp4[:, 1, :, :], tmp4[:, 0, :, :], ACT.Exp).then_inc(cw_exp, 1)
                        act.wait_ge(f_full, n + 1)
                        if n >= 2:
                            act.wait_ge(g_ready, 2 * (n - 1))
                        act.activation(g32[:, n % 2, :], ps[:, 4 + n % 3, :], gelu,
                                                       bias=b1col[:, e, ft:ft + 1]).then_inc(f_free, 1)
                phase_end(act)

        @block.tensor
        def _(pe):
            mm = pe.matmul
            KD = (128, 128, 32)

            pe.wait_ge(p_in, 96)
            for c in range(3):
                ins = mm(ps[0:D, 0, 0:D], Psb[0:KD[c], c, :], Psb[0:KD[c], c, :], start=c == 0, stop=c == 2)
            ins.then_inc(gram, 1)
            pe.wait_ge(consts, 6)

            def spread_gram(j):
                pe.wait_ge(gi_upd, j + 1)
                if j >= 2:
                    pe.wait_ge(n2_ready, j - 1)
                k = j % 2
                mm(ps[0:D, k, 0:2 * D], ident[0:D, j:j + 1].broadcast_to([D, D]), GI[:, :],
                                 start=True, stop=True).then_inc(bc_g, 1)

            def spread_top(j):
                if j > 0:
                    pe.wait_ge(t_upd, j)
                k = j % 2
                mm(ps[0:D, 2 + k, 0:D], ident[0:D, j:j + 1].broadcast_to([D, D]), T[:, :],
                                 start=True, stop=True).then_inc(bc_t, 1)

            def x_transpose(b, c):
                n = 3 * b + c
                pe.wait_ge(x_in, 16 * B)
                if n > 0:
                    pe.wait_ge(xt_ev, n)
                for t in range(TT):
                    ins = pe.transpose(ps[0:KD[c], 4, 128 * t:128 * t + 128], X[:, TT * b + t, 128 * c:128 * c + KD[c]],
                                       ident[:, :])
                ins.then_inc(xt_mm, 1)

            def y_product(b):
                pe.wait_ge(xt_ev, 3 * b + 3)
                if b > 0:
                    pe.wait_ge(y_ev, b)
                for c in range(3):
                    ins = mm(ps[0:D, 5, :], Psb[0:KD[c], c, :], XT[0:KD[c], c, :], start=c == 0, stop=c == 2)
                ins.then_inc(y_mm, 1)

            def skew_columns(j0, j1):
                pe.wait_ge(w_in, 32)
                pe.wait_ge(silu_done, 1)
                pe.wait_ge(skew_zero, 1)
                o = ps[0:D, 6, 0:B * D].rearrange("p (b j) -> p b j", b=B)
                for j in range(j0, j1):
                    at = j * (j - 1) // 2
                    for c in range(3):
                        ins = mm(o[0:j, :, j], Wsk[0:KD[c], c, at:at + j], csil[0:KD[c], c, :], start=c == 0, stop=c == 2)
                if j1 == D:
                    ins.then_inc(skew_mm, 1)

            def skew_transpose():
                pe.wait_ge(up_ready, 1)
                for b in range(B):
                    ins = pe.transpose(ps[0:D, 7, D * b:D * b + D], Up[:, b, :], ident[0:D, 0:D])
                ins.then_inc(skew_t, 1)

            def exp_half(r, x):
                if r == 0:
                    pe.wait_ge(skew_done, 4)
                else:
                    pe.wait_ge(exp_ev, r)
                cur = EF[:, r % 2]
                for b in range(B):
                    at = 256 * x + D * b
                    left = BB[:, 1 - x, b, :] if r < DEGREE - 1 else cur[:, 1 - x, b, :]
                    one = ident[0:D, 0:D] if r < DEGREE - 1 else ident2[:, :]
                    o = ps[0:D, 6, at:at + D]
                    mm(o, left, cur[:, x, b, :], start=True, stop=False)
                    ins = mm(o, left, one, start=False, stop=True)
                ins.then_inc(exp_mm, 1)

            def ada_products(l):
                pe.wait_ge(ada_in[l], 32)
                pe.wait_ge(silu_done, 1)
                pe.wait_ge(y_ev, B)
                pe.wait_ge(skew_done, 4)
                if l > 0:
                    pe.wait_ge(ada_ev, 5 * l)
                vec = (0, 1, 3, 4)
                for c in range(3):
                    for v in range(4):
                        for r in range(1 if c < 2 else 3):
                            rows = 128 if c < 2 else 32
                            at = C * vec[v] + 128 * c
                            for k in range(3):
                                mm(ps[32 * r:32 * r + rows, 4, B * (4 * c + v):B * (4 * c + v) + B],
                                   WA[0:KD[k], l, k, at:at + rows], csil[0:KD[k], k, :], start=k == 0, stop=k == 2)
                for i, bank in ((0, 5), (1, 7)):
                    for k in range(3):
                        ins = mm(ps[0:B, bank, 0:C], csil[0:KD[k], k, :], WA[0:KD[k], l, k, C * (2 + 3 * i):C * (3 + 3 * i)],
                                 start=k == 0, stop=k == 2)
                ins.then_inc(ada_mm, 1)

            halves = [(r, x) for r in range(ROUNDS) for x in range(2)]
            for j in range(D):
                spread_gram(j)
                spread_top(j)
                if 3 <= j < 19:
                    b, c = divmod(j - 3, 4)
                    x_transpose(b, c) if c < 3 else y_product(b)
                if 19 <= j < 28:
                    skew_columns(max(1, 7 * (j - 19)), 7 * (j - 18) if j < 27 else D)
                if j == 28:
                    skew_transpose()
                if j >= 30:
                    exp_half(*halves[j - 30])
                if j in ADA_AT:
                    ada_products(ADA_AT.index(j))
            for r, x in halves[D - 30:]:
                exp_half(r, x)
            pe.wait_ge(rt_ready, 1)
            pe.wait_ge(exp_ev, ROUNDS)
            for b in range(B):
                ins = mm(ps[0:D, 0, D * b:D * b + D], EF[:, ROUNDS % 2, 1, b, :], RT[:, :], start=True, stop=True)
            ins.then_inc(mid_mm, 1)
            pe.wait_ge(mid_ev, 1)
            mm(ps[0:D, 1, 0:B * D], RT[:, :], X1[:, :, :].rearrange("p b j -> p (b j)"), start=True, stop=True).then_inc(mid_mm, 1)
            pe.wait_ge(mid_ev, 2)
            pe.wait_ge(ada_ev, 5 * LAYERS)
            for b in range(B + 1):
                if b < B:
                    if b >= 2:
                        pe.wait_ge(ym_ev, b - 1)
                    mm(ps[0:D, 2 + b % 2, :], Mid[:, b, :], YT[:, b, :], start=True, stop=True).then_inc(ym_mm, 1)
                if b > 0:
                    pe.wait_ge(ym_ev, b)
                    for t in range(TT):
                        n = TT * (b - 1) + t
                        if n >= TT:
                            pe.wait_ge(l0_done, n - TT + 1)
                        mm(ps[:, 4 + t, 0:C], YM[:, (b - 1) % 2, 128 * t:128 * t + 128], PT[:, :],
                                          start=True, stop=True).then_inc(l0_mm, 1)
            phase_end(pe)

            def seven(o, lhs, rhs):
                for p in range(7):
                    w, h = PASSES[p]
                    ins = mm(o, lhs(w, h, KROWS[w]), rhs(w, h, KROWS[w]), start=p == 0, stop=p == 6)
                return ins

            for l in range(LAYERS):
                M, W = MISC[l], NORM[l]
                phase_begin(pe, 2 * l + 1)
                pe.wait_ge(wp_in, 96 * (l + 1))

                def work(kind, i, k):
                    n = M[kind, i, k]
                    if n > 0:
                        pe.wait_ge(misc_free, n)
                    bank = ps[:, 7, :]
                    if kind == "ln":
                        pe.wait_ge(xn_ready, 4 * (8 * l + i + 1))
                        rows = 128 if k < 2 else 96
                        for t in range(TT):
                            ins = pe.transpose(bank[0:rows, 128 * t:128 * t + 128], xn[:, t, 128 * k:128 * k + rows], ident[:, :])
                    elif kind in ("q", "k") and l == 1:
                        qk = "qk".index(kind)
                        pe.wait_ge(qn_ready, 2 * i + qk + 1)
                        src = rowt if qk else QN
                        for t in range(TT):
                            ins = pe.transpose(bank[0:MROWS[k], 128 * t:128 * t + 128], src[:, t, 126 * k:126 * k + MROWS[k]],
                                               ident[:, :])
                    elif kind in ("q", "k"):
                        pe.wait_ge(act_split, 3 * (4 * l + i) + 3)
                        pe.wait_ge(wq_split, 3 * (l + 1))
                        at = C * "qk".index(kind) + 126 * k
                        ins = seven(bank[0:MROWS[k], :], lambda w, h, r: WQ[0:r, w, at:at + MROWS[k]],
                                    lambda w, h, r: HQ[0:r, h, :])
                    elif kind in ("v", "qtok", "ktok"):
                        pe.wait_ge(act_split, 3 * (4 * l + i) + 3)
                        pe.wait_ge(wq_split, 3 * (l + 1))
                        at = C * "qkv".index(kind[0])
                        ins = seven(bank[:, 0:C], lambda w, h, r: HQ[0:r, h, 128 * k:128 * k + 128],
                                    lambda w, h, r: WQ[0:r, w, at:at + C])
                    elif kind == "max":
                        pe.wait_ge(a_free, 16 * (STEPS * l + i + 1))
                        for t in range(TT):
                            ins = pe.transpose(bank[0:4, 128 * t:128 * t + 128], negmax[:, i % 2, t, :], ident[:, :])
                    elif kind == "sum":
                        pe.wait_ge(o_out, STEPS * l + i + 1)
                        for t in range(TT):
                            ins = mm(bank[:, 4 * t:4 * t + 4], oT[:, i % 5, 128 * t:128 * t + 128], pick[:, :], start=True, stop=True)
                    elif kind == "inv":
                        for t in range(TT):
                            for j in range(4):
                                ins = mm(bank[32 * j:32 * j + 32, 128 * t:128 * t + 128],
                                         rsum[:, t, j:j + 1].broadcast_to([128, 32]), ident[:, :], start=True, stop=True)
                    elif kind == "proj":
                        pe.wait_ge(misc_free, M["inv", 4 * i + 3, 0] + 1)
                        for g in range(4):
                            ins = mm(bank[:, 0:C], oT[:, (4 * i + g) % 5, 128 * k:128 * k + 128], WP[:, g, :],
                                     start=g == 0, stop=g == 3)
                    ins.then_inc(misc_full, 1)

                def query_scores(s, i):
                    n = 16 * (STEPS * l + s) + i
                    h = 4 * (s % 4) + i // 4
                    if i % 4 == 0:
                        pe.wait_ge(qk_in[POSITION[h]], 96 * (4 * l + s // 4 + 1))
                    if n >= 2:
                        pe.wait_ge(a_free, n - 1)
                    t = i % 4
                    mm(ps[:, 4 + i % 2, :], Q3[0:QK_ROWS, h, 128 * t:128 * t + 128], K3[0:QK_ROWS, h, :],
                                       start=True, stop=True).then_inc(a_full, 1)

                def key_scores(s, u):
                    n = 8 * (STEPS * l + s) + u
                    if u == 0:
                        pe.wait_ge(mrow_in, 64 * (STEPS * l + s + 1))
                    if n >= 2:
                        pe.wait_ge(b_free, n - 1)
                    t = u // 2
                    for i in range(2):
                        h = 4 * (s % 4) + 2 * (u % 2) + i
                        ins = mm(ps[:, 2 * (u % 2) + i, :], K3[0:QROW + 1, h, 128 * t:128 * t + 128], Q3[0:QROW + 1, h, :],
                                 start=True, stop=True)
                    ins.then_inc(b_full, 1)

                def values(s, t):
                    n = STEPS * l + s
                    pe.wait_ge(b_free, 8 * n + 2 * t + 2)
                    if t == 0:
                        pe.wait_ge(misc_free, M["v", s // 4, TT - 1] + 1)
                        if n > 0:
                            pe.wait_ge(o_out, n)
                    for i in range(4):
                        at = VW * (4 * (s % 4) + i)
                        ins = mm(ps[32 * i:32 * i + 32, 6, :], V[:, s // 4 % 2, t, at:at + 32], Pr[:, t % 2, i, :],
                                 start=t == 0, stop=t == TT - 1)
                    ins.then_inc(av_done, 1)

                for key in prologue(l):
                    if key[0] in BANK:
                        work(*key)
                for i in range(16):
                    query_scores(0, i)
                work("max", 0, 0)
                for i in range(16):
                    query_scores(1, i)
                for s in range(STEPS):
                    for u in range(8):
                        for at, *key in plan(l, s):
                            if at == u and key[0] in BANK:
                                work(*key)
                        key_scores(s, u)
                        if s + 2 < STEPS:
                            query_scores(s + 2, 2 * u)
                            query_scores(s + 2, 2 * u + 1)
                        if u == 1 and s > 0:
                            values(s - 1, TT - 1)
                        if u % 2 and u >= 3:
                            values(s, (u - 3) // 2)
                values(STEPS - 1, TT - 1)
                for key in MISC_EPILOGUE:
                    work(*key)
                phase_end(pe)

                phase_begin(pe, 2 * l + 2)
                E = EXPERTS[l]

                def norm_work(kind, b, c):
                    n = W[kind, b, c]
                    if n > 0:
                        pe.wait_ge(norm_free, n)
                    if kind == "ln":
                        pe.wait_ge(xn_ready, 4 * (8 * l + 4 + b + 1))
                        rows = 128 if c < 2 else 96
                        for t in range(TT):
                            ins = pe.transpose(ps[0:rows, 7, 128 * t:128 * t + 128], xn[:, t, 128 * c:128 * c + rows], ident[:, :])
                    else:
                        pe.wait_ge(hm_ready, 3 * (4 * l + b) + 3)
                        pe.wait_ge(wg_split, 3)
                        for t in range(TT):
                            ins = seven(ps[:, 7, 4 * t:4 * t + 4], lambda w, h, r: HM[0:r, b, h, 128 * t:128 * t + 128],
                                        lambda w, h, r: Wg[0:r, w, :])
                    ins.then_inc(norm_full, 1)

                def hidden(e, b, ft):
                    n, k = FT * (B * (EBASE[l] + e) + b) + ft, (EBASE[l] + e) % 2
                    if ft == 0:
                        pe.wait_ge(hm_ready, 3 * (4 * l + b) + 3)
                        pe.wait_ge(w_split, 12 * (EBASE[l] + e) + 6)
                    if n >= 3:
                        pe.wait_ge(f_free, n - 2)
                    seven(ps[:, 4 + n % 3, :], lambda w, h, r: W1[0:r, k, w, 128 * ft:128 * ft + 128],
                                          lambda w, h, r: HM[0:r, b, h, :]).then_inc(f_full, 1)

                def back(e, b, ft):
                    U, k = B * (EBASE[l] + e) + b, (EBASE[l] + e) % 2
                    n = FT * U + ft
                    pe.wait_ge(g_ready, 2 * (n + 1))
                    if ft == 0:
                        pe.wait_ge(w_split, 12 * (EBASE[l] + e) + 12)
                    for t in range(TT):
                        if ft == 0 and U > 0:
                            pe.wait_ge(acc_free, TT * (U - 1) + t + 1)
                        for p, (x, w) in enumerate(((0, 0), (1, 0), (0, 1))):
                            ins = mm(ps[:, t, 0:C], G[:, n % 3, x, 128 * t:128 * t + 128], W2[:, k, w, ft, :],
                                     start=ft == 0 and p == 0, stop=ft == FT - 1 and p == 2)
                        if ft == FT - 1:
                            ins.then_inc(acc_full, 1)
                    if ft < FT - 1:
                        ins.then_inc(g_used, 1)

                for c in range(3):
                    norm_work("ln", 0, c)
                tiles = [(e, b, ft) for e in range(E) for b in range(B) for ft in range(FT)]
                for v, (e, b, ft) in enumerate(tiles):
                    if e == 0:
                        for key in norm_plan(l, b, ft):
                            norm_work(*key)
                    hidden(e, b, ft)
                    if v >= 2:
                        back(*tiles[v - 2])
                back(*tiles[-2])
                back(*tiles[-1])
                phase_end(pe)


ADA_AT = (44, 52, 60)

_INS = (["x", "P", "PT", "Wsk", "bsk", "cond", "ada_bcol", "ada_brow", "ada_w", "w_qkv", "w_proj", "qkcol", "vrow",
         "prow", "qkrow", "w_gate"] + [f"{n}_{l}" for l in range(LAYERS) for n in ("w1", "b1", "w2", "b2")])


def layout(inputs):
    g = {k: np.asarray(v) for k, v in inputs.items()}
    L = (dict(ada="L1_cond_W_ada", ba="L1_cond_b_ada", wq="L1_cond_W_qkv", bq="L1_cond_b_qkv", wp="L1_cond_W_proj",
              bp="L1_cond_b_proj", w1="L1_cond_W_fc1", b1="L1_cond_b_fc1", w2="L1_cond_W_fc2", b2="L1_cond_b_fc2"),
         dict(ada="L2_cond_w_ada", ba="L2_cond_b_ada", wq="L2_cond_w_qkv", bq="L2_cond_b_qkv", wp="L2_cond_w_proj",
              bp="L2_cond_b_proj", w1="L2_cond_w1", b1="L2_cond_b1", w2="L2_cond_w2", b2="L2_cond_b2"),
         dict(ada="L3_cond_w_adaln", ba="L3_cond_b_adaln", wq="L3_cond_w_qkv", bq="L3_cond_b_qkv",
              wp="L3_cond_w_proj", bp="L3_cond_b_proj", w1="L3_cond_w1", b1="L3_cond_b1", w2="L3_cond_w2",
              b2="L3_cond_b2"))
    f32 = np.float32
    o = {"x": g["x"], "P": g["L0_cond_P"], "PT": g["L0_cond_P"].T}
    iu, ju = np.triu_indices(D, k=1)
    by_column = np.lexsort((iu, ju))
    o["Wsk"] = g["L0_cond_W"][by_column].T
    o["bsk"] = np.zeros((D, D), f32)
    o["bsk"][iu, ju] = g["L0_cond_b"]
    o["cond"] = np.zeros((128, 3, B), f32)
    for c, rows in enumerate((128, 128, 32)):
        o["cond"][:rows, c, :] = g["cond_1152"].T[128 * c:128 * c + rows]
    heads = np.array([HD * h + d for h in ORDER for d in range(HD)])
    o["ada_bcol"] = np.zeros((128, LAYERS, 3, 4), f32)
    o["ada_brow"] = np.zeros((LAYERS, 2, C), f32)
    o["ada_w"] = np.zeros((LAYERS, C, 6 * C), f32)
    o["w_qkv"] = np.zeros((LAYERS, C, 3 * C), f32)
    o["w_proj"] = np.zeros((LAYERS, 128, 4, C), f32)
    o["qkcol"] = np.zeros((LAYERS, 126, 2, NM, 2), f32)
    o["vrow"] = np.zeros((LAYERS, C), f32)
    o["prow"] = np.zeros((LAYERS, C), f32)
    o["qkrow"] = np.zeros((LAYERS, 2, C), f32)
    for l in range(LAYERS):
        n = L[l]
        six = g[n["ba"]].reshape(6, C)
        for v, k in enumerate((0, 1, 3, 4)):
            for c in range(2):
                o["ada_bcol"][:, l, c, v] = six[k, 128 * c:128 * c + 128]
            for r in range(3):
                o["ada_bcol"][32 * r:32 * r + 32, l, 2, v] = six[k, 256:]
        o["ada_brow"][l, 0], o["ada_brow"][l, 1] = six[2], six[5]
        o["ada_w"][l] = g[n["ada"]]
        wq, bq = g[n["wq"]], g[n["bq"]]
        o["w_qkv"][l, :, :2 * C] = wq[:, :2 * C]
        o["w_qkv"][l, :, 2 * C:] = wq[:, 2 * C:][:, heads]
        o["vrow"][l] = bq[2 * C:][heads]
        for i, h in enumerate(ORDER):
            o["w_proj"][l, 32 * (i % 4):32 * (i % 4) + HD, i // 4, :] = g[n["wp"]][HD * h:HD * h + HD]
        o["prow"][l] = g[n["bp"]]
        for qk in range(2):
            for m in range(NM):
                r = MROWS[m]
                if l == 1:
                    o["qkcol"][l, :r, qk, m, 0] = np.tile(g["L2_cond_qn_g" if qk == 0 else "L2_cond_kn_g"], r // HD)
                    o["qkcol"][l, :r, qk, m, 1] = np.tile(g["L2_cond_qn_b" if qk == 0 else "L2_cond_kn_b"], r // HD)
                else:
                    o["qkcol"][l, :r, qk, m, 1] = bq[C * qk + 126 * m:C * qk + 126 * m + r]
            o["qkrow"][l, qk] = bq[C * qk:C * qk + C]
        E = EXPERTS[l]
        o[f"w1_{l}"] = g[n["w1"]].reshape(E, C, FF)
        o[f"w2_{l}"] = g[n["w2"]].reshape(E, FF, C)
        o[f"b1_{l}"] = g[n["b1"]].reshape(E, FT, 128).transpose(2, 0, 1)
        o[f"b2_{l}"] = g[n["b2"]].reshape(E, C)
    o["w_gate"] = g["L3_cond_w_gate"]
    return {k: np.ascontiguousarray(v) for k, v in o.items()}


def kernel(**inputs):
    import concourse.bacc as bacc
    from concourse.bass_utils import run_bass_kernel_spmd

    nc = bacc.Bacc("TRN2", target_bir_lowering=False, num_devices=1)
    data = layout(inputs)
    arrays = {f"in_{k}": data[k] for k in _INS}
    aps = {k: nc.dram_tensor(f"in_{k}", data[k].shape, F32, kind="ExternalInput").ap() for k in _INS}
    result = nc.dram_tensor("out_0", (B, N, C), F32, kind="ExternalOutput").ap()
    build(nc, aps, result)
    r = run_bass_kernel_spmd(nc, [arrays], core_ids=[0])
    return r.results[0]["out_0"]
```

```python
from contextlib import ExitStack

import numpy as np
import concourse.bass as bass
from concourse import mybir

F32 = mybir.dt.float32
F32R = mybir.dt.float32r
ALU = mybir.AluOpType
ACT = mybir.ActivationFunctionType
AX = mybir.AxisListType.X

B, N, C = 4, 512, 288
H, HD = 16, 18
FF = 4 * C
D = 64
LAYERS = 3
EXPERTS = (1, 1, 4)
TT = N // 128
FT = FF // 128
NM = 3
MROWS = (126, 126, 36)
SCALE = float(HD) ** -0.5
LN_EPS, QK_EPS = 1e-6, 1e-5
VW = HD + 1
ORDER = [7 * m + j for j in range(7) for m in range(NM) if 7 * m + j < H]
START = [ORDER.index(j) for j in range(7)]
WIDTH = [len([m for m in range(NM) if 7 * m + j < H]) for j in range(7)]
POSITION = [j for j in range(7) for _ in range(WIDTH[j])]
PASSES = ((0, 0), (1, 1), (0, 2), (1, 3), (2, 0), (3, 1), (4, 4))
KROWS = (128, 128, 128, 128, 96)
QR0, QR1, QR2, QROW, QK_ROWS = 0, 32, 64, 82, 82
STEPS = 4 * B
SQUARINGS, DEGREE = 14, 6
ROUNDS = DEGREE - 1 + SQUARINGS
EBASE = [sum(EXPERTS[:l]) for l in range(LAYERS + 1)]


BANK = ("ln", "q", "k", "v", "qtok", "ktok", "max", "proj")
PLAIN = (
    [(2, "ln", 1, 2), (4, "q", 1, 0), (5, "q", 1, 1), (6, "q", 1, 2), (7, "k", 1, 0)],
    [(0, "k", 1, 1), (3, "k", 1, 2), (4, "proj", -1, 0), (6, "proj", -1, 1)],
    [(0, "proj", -1, 2), (2, "proj", -1, 3), (4, "v", 1, 0), (6, "v", 1, 1)] + [(4 + t, "stats", 2, t) for t in range(TT)],
    [(0, "v", 1, 2), (0, "mean", 2, 0), (2, "v", 1, 3), (2, "scale", 2, 0), (3, "scale", 2, 1), (4, "ln", 2, 0),
     (6, "ln", 2, 1)])
NORMED = (
    [(1, "kvar", 1, 1), (3, "ktok", 1, 2), (4, "q", 1, 0), (5, "kvar", 1, 2), (5, "ktok", 1, 3), (5, "q", 1, 1),
     (6, "q", 1, 2), (7, "kvar", 1, 3), (7, "proj", -1, 0)],
    [(t, "stats", 2, t) for t in range(TT)] +
    [(0, "proj", -1, 1), (2, "k", 1, 0), (3, "k", 1, 1), (4, "k", 1, 2), (5, "proj", -1, 2), (4, "mean", 2, 0),
     (6, "v", 1, 0), (6, "v", 1, 1), (5, "scale", 2, 0), (7, "v", 1, 2), (7, "v", 1, 3), (6, "scale", 2, 1)],
    [(0, "proj", -1, 3), (0, "ln", 2, 0), (2, "ln", 2, 1), (3, "ln", 2, 2), (4, "qtok", 2, 0), (6, "qvar", 2, 0), (6, "qtok", 2, 1)],
    [(0, "qvar", 2, 1), (0, "qtok", 2, 2), (2, "qvar", 2, 2), (3, "qtok", 2, 3), (5, "qvar", 2, 3), (5, "ktok", 2, 0), (7, "kvar", 2, 0),
     (7, "ktok", 2, 1)])


def plan(layer, s):
    b, g = divmod(s, 4)
    out = [(1, "max", s + 1, 0)] if s + 1 < STEPS else []
    if s > 0:
        out += [(u, "out", s - 1, k) for k, u in enumerate((1, 2, 2, 3))]
    if s == STEPS - 2:
        out += [(2 * t, "stats2", 0, t) for t in range(TT)]
    if s == STEPS - 1:
        out += [(0, "mean2", 0, 0), (4, "scale2", 0, 0), (5, "scale2", 0, 1)]
    out += [(u, kind, b + d, k) for u, kind, d, k in (NORMED if layer == 1 else PLAIN)[g] if 0 <= b + d < B]
    return sorted(out, key=lambda x: x[0])


def prologue(layer):
    def norm(b):
        return [("stats", b, t) for t in range(TT)] + [("mean", b, 0), ("scale", b, 0), ("scale", b, 1)]

    out = (norm(0) if layer == 0 else []) + [("split", 0, 0)] + [("ln", 0, c) for c in range(3)] + [("zero", 0, 0)]
    if layer == 1:
        out += [(qk + kind, 0, t) for qk in "qk" for t in range(TT) for kind in ("tok", "var")]
    else:
        out += norm(1)
    out += [(qk, 0, i) for qk in "qk" for i in range(NM)] + [("v", 0, t) for t in range(TT)]
    return out + (norm(1) if layer == 1 else [])


def warm_up(layer):
    out = [(17, "max", 0, 0)] + [(2 + 2 * c, "ln", 1, c) for c in range(3 if layer == 1 else 2)]
    if layer == 1:
        at = 9
        for kind, t in [("q", t) for t in range(TT)] + [("k", 0), ("k", 1)]:
            out.append((at, kind + "tok", 1, t))
            at += 3
            if (kind, t) != ("k", 1):
                out.append((at, kind + "var", 1, t))
    return sorted(out, key=lambda x: x[0])


EPILOGUE = [("out", STEPS - 1, k) for k in range(4)] + [("proj", B - 1, t) for t in range(TT)]


def all_order(layer):
    seq = prologue(layer) + [x[1:] for x in warm_up(layer)]
    for s in range(STEPS):
        seq += [x[1:] for x in plan(layer, s)]
    return seq + EPILOGUE


def misc_order(layer):
    return [key for key in all_order(layer) if key[0] in BANK]


def norm_plan(layer, b, f):
    if f == 1 and EXPERTS[layer] > 1:
        return [("gate", b, 0)]
    if f >= 6 and b + 1 < B:
        return [("ln", b + 1, f - 6)]
    return []


def norm_order(layer):
    seq = [("ln", 0, c) for c in range(3)]
    for b in range(B):
        for f_ in range(FT):
            seq += norm_plan(layer, b, f_)
    return seq


def number(orders):
    out, n = [], 0
    for seq in orders:
        out.append({key: n + i for i, key in enumerate(seq)})
        n += len(seq)
    return out


def build(nc, a, out):
    with ExitStack() as ctx:
        def sb(name, shape, dt=F32, where=ctx):
            return where.enter_context(nc.sbuf_tensor(name, shape, dt))

        ps = ctx.enter_context(nc.psum_tensor("ps", [128, 8, 512], F32))
        gate_rows = nc.dram_tensor("gate_rows", (LAYERS, B, 2, C), F32).ap()

        X = sb("X", [128, B * TT, C])
        ident = sb("ident", [128, 128])
        ada = sb("ada", [128, LAYERS, 3, 4, B])
        stats = sb("stats", [128, TT, 6])
        mv = sb("mv", [128, TT, 2])
        var4 = sb("var4", [128, TT])
        rowt0 = sb("rowt0", [128, TT])
        rstd = sb("rstd", [128, TT])
        neghalf = sb("neghalf", [128, H])
        xn = sb("xn", [128, TT, C + 64])
        act32 = sb("act32", [128, 2, N])
        gbc = sb("gbc", [128, B, C])
        rowt = sb("rowt", [128, TT, C])

        p0 = ExitStack()
        Psb = sb("Psb", [128, 3, D], F32, p0)
        PTz = sb("PT", [128, C], F32, p0)
        PT = PTz[0:D, :]
        Wsk = sb("Wsk", [128, 3, D * (D - 1) // 2], F32, p0)
        bsk = sb("bsk", [D, D], F32, p0)
        ccol = sb("ccol", [128, 3, B], F32, p0)
        cexp = sb("cexp", [128, 3, B], F32, p0)
        csil = sb("csil", [128, 3, B], F32, p0)
        WA = sb("WA", [128, LAYERS, 3, 6 * C], F32, p0)
        bacol = sb("bacol", [128, LAYERS, 3, 4], F32, p0)
        barow = sb("barow", [B, LAYERS, 2, C], F32, p0)
        grow = sb("grow", [B, LAYERS, 2, C], F32, p0)
        Tz = sb("T", [128, D], F32, p0)
        T = Tz[0:D, :]
        GIz = sb("GI", [128, 2 * D], F32, p0)
        GI = GIz[0:D, :]
        below = sb("below", [D, D], F32, p0)
        RG = sb("RG", [D, 2, D], F32, p0)
        NB = sb("NB", [D, D], F32, p0)
        small = sb("small", [D, 2, 8], F32, p0)
        plushalf = sb("plushalf", [D, 1], F32, p0)
        RT = sb("RT", [D, D], F32, p0)
        Up = sb("Up", [D, B, D], F32, p0)
        BBz = sb("BB", [128, 2, B, D], F32, p0)
        EFz = sb("EF", [128, 2, 2, B, D], F32, p0)
        BB, EF = BBz[0:D], EFz[0:D]
        ident2 = sb("ident2", [128, D], F32, p0)
        XT = sb("XT", [128, 3, N], F32, p0)
        YTz = sb("YT", [128, B, N], F32, p0)
        YT = YTz[0:D]
        X1 = sb("X1", [D, B, D], F32, p0)
        Midz = sb("Mid", [128, B, D], F32, p0)
        YMz = sb("YM", [128, 2, N], F32, p0)
        Mid, YM = Midz[0:D], YMz[0:D]
        p0.close()

        pa = ExitStack()
        Q3 = sb("Q3", [100, H, N], F32R, pa)
        mrow = Q3[96:100, 0, :]
        K3 = sb("K3", [96, H, N], F32R, pa)
        stage = sb("stage", [126, 2, 2, NM, N], F32R, pa)
        Pr = sb("Pr", [128, 2, 4, N], F32, pa)
        V = sb("V", [128, 2, TT, 320], F32, pa)
        HQ = sb("HQ", [128, 5, N], F32R, pa)
        WQ = sb("WQ", [128, 5, 3 * C], F32R, pa)
        WP = sb("WP", [128, 4, C], F32, pa)
        oT = sb("oT", [128, 5, N], F32, pa)
        oTok = sb("oTok", [128, 16, 32], F32, pa)
        rsum = sb("rsum", [128, 16], F32, pa)
        ptmp = sb("ptmp", [128, C], F32, pa)
        squares = sb("squares", [128, C], F32, pa)
        qkcol = sb("qkcol", [126, 2, NM, 2], F32, pa)
        vrow = sb("vrow", [128, C], F32, pa)
        prow = sb("prow", [128, C], F32, pa)
        negmax = sb("negmax", [128, 2, TT, 4], F32, pa)
        QN = sb("QN", [128, TT, C], F32, pa)
        qkrow = sb("qkrow", [128, 2, C], F32, pa)
        qstat = sb("qstat", [128, 4, TT, H], F32, pa)
        pa.close()
        RawQ = Pr[:, :, :, :].rearrange("p a h n -> p (a h n)")[:, 0:9 * C].rearrange("p (s n) -> p s n", s=3)

        pm = ExitStack()
        HM = sb("HM", [128, B, 5, N], F32R, pm)
        W1 = sb("W1", [128, 2, 5, FF], F32R, pm)
        W2 = sb("W2", [128, 2, 2, FT, C], F32R, pm)
        raw = sb("raw", [128, 3, FF], F32, pm)
        g32 = sb("g32", [128, 2, N], F32, pm)
        G = sb("G", [128, 3, 2, N], F32R, pm)
        b1col = sb("b1col", [128, 4, FT], F32, pm)
        b2row = sb("b2row", [128, 4, C], F32, pm)
        Wg = sb("Wg", [128, 5, 4], F32R, pm)
        rawg = sb("rawg", [128, 3, 4], F32, pm)
        lg = sb("lg", [128, TT, 4], F32, pm)
        wins = sb("wins", [128, TT, 6], F32, pm)
        tmp4 = sb("tmp4", [128, 2, TT, 4], F32, pm)
        chosen = sb("chosen", [128, TT, 4], F32, pm)
        top = sb("top", [128, 2, TT], F32, pm)
        cw = sb("cw", [128, B, TT, 4], F32, pm)
        pm.close()

        def sem(name):
            return ctx.enter_context(nc.semaphore(name))

        x_in = sem("x_in")
        p_in = sem("p_in")
        w_in = sem("w_in")
        ada_b_in = sem("ada_b_in")
        ada_in = [sem(f"ada_in{l}") for l in range(LAYERS)]
        consts = sem("consts")
        pads = sem("pads")
        silu_exp = sem("silu_exp")
        silu_done = sem("silu_done")
        bc_g = sem("bc_g")
        bc_t = sem("bc_t")
        gi_upd = sem("gi_upd")
        t_upd = sem("t_upd")
        n2_ready = sem("n2_ready")
        n2_root = sem("n2_root")
        dve_done = sem("dve_done")
        pool_done = sem("pool_done")
        skew_zero = sem("skew_zero")
        skew_mm = sem("skew_mm")
        up_ready = sem("up_ready")
        skew_t = sem("skew_t")
        skew_done = sem("skew_done")
        exp_mm = sem("exp_mm")
        exp_ev = sem("exp_ev")
        rt_ready = sem("rt_ready")
        xt_mm = sem("xt_mm")
        xt_ev = sem("xt_ev")
        y_mm = sem("y_mm")
        y_ev = sem("y_ev")
        mid_mm = sem("mid_mm")
        mid_ev = sem("mid_ev")
        ym_mm = sem("ym_mm")
        ym_ev = sem("ym_ev")
        l0_mm = sem("l0_mm")
        l0_done = sem("l0_done")
        ada_mm = sem("ada_mm")
        ada_ev = sem("ada_ev")
        gate_out = sem("gate_out")
        gram = sem("gram")
        wq_in = sem("wq_in")
        wq_split = sem("wq_split")
        wp_in = sem("wp_in")
        gate_in = sem("gate_in")
        var_ready = sem("var_ready")
        rstd_ready = sem("rstd_ready")
        xn_ready = sem("xn_ready")
        misc_full = sem("misc_full")
        misc_free = sem("misc_free")
        act_split = sem("act_split")
        a_full = sem("a_full")
        a_free = sem("a_free")
        b_full = sem("b_full")
        b_free = sem("b_free")
        av_done = sem("av_done")
        o_out = sem("o_out")
        o_rec = sem("o_rec")
        o_mul = sem("o_mul")
        ot_ready = sem("ot_ready")
        mrow_in = sem("mrow_in")
        staged = sem("staged")
        qk_var = sem("qk_var")
        qk_sum = sem("qk_sum")
        qk_sq = sem("qk_sq")
        qk_root = sem("qk_root")
        qn_ready = sem("qn_ready")
        att_zero = sem("att_zero")
        w_raw = [sem(f"w_raw{k}") for k in range(3)]
        w_split = sem("w_split")
        wg_in = sem("wg_in")
        wg_split = sem("wg_split")
        f_full = sem("f_full")
        f_free = sem("f_free")
        g_ready = sem("g_ready")
        g_used = sem("g_used")
        acc_full = sem("acc_full")
        acc_free = sem("acc_free")
        norm_full = sem("norm_full")
        norm_free = sem("norm_free")
        hm_ready = sem("hm_ready")
        logits = sem("logits")
        cw_exp = sem("cw_exp")
        phase_over = sem("phase_over")
        out_done = sem("out_done")
        qk_in = [sem(f"qk_in{j}") for j in range(7)]
        MISC = number([misc_order(l) for l in range(LAYERS)])
        NORM = number([norm_order(l) for l in range(LAYERS)])
        held = []
        for l in range(LAYERS):
            held += [(l, "att", *k) for k in misc_order(l) if k[0] in ("ln", "q", "k")]
            held += [(l, "mlp", *k) for k in norm_order(l) if k[0] == "ln"]
        HELD = {k: i for i, k in enumerate(held)}

        def shared(l, key):
            first = [k for k in prologue(l) if k[0] in BANK]
            return 6 if tuple(key) in first and first.index(tuple(key)) % 2 else 7

        steps = [0]

        def step():
            steps[0] += 1
            return steps[0]

        pool_steps = [0]

        def pool_step():
            pool_steps[0] += 1
            return pool_steps[0]

        def phase_begin(eng, k):
            eng.wait_ge(phase_over, 5 * k)

        def phase_end(eng):
            eng.sem_inc(phase_over, 1)

        def parts(dst, c):
            if c < 2:
                return dst[:, c, :], dst[:, 2 + c, :], slice(0, 128)
            return dst[0:96, 4, :], dst[32:64, 4, :], slice(32, 64)

        def low_of(eng, kind, i, k, h):
            if kind == "ln":
                hi, lo, rows = parts(HQ, k)
                high = hi if k < 2 else HQ[32:64, 4, :]
                return eng.tensor_tensor(lo, act32[rows, h % 2, :], high.bitcast(F32), ALU.subtract)
            rows, qk = MROWS[k], "qk".index(kind)
            return eng.tensor_tensor(stage[0:rows, qk, 1, k, :], act32[0:rows, h % 2, :],
                                     stage[0:rows, qk, 0, k, :].bitcast(F32), ALU.subtract)

        def two_banks(l, key):
            first = [k for k in prologue(l) if k[0] in BANK]
            return key in first[1:] and all(k[0] in ("ln", "q", "k") for k in (key, first[first.index(key) - 1]))

        def low_engine(l, kind, i):
            return "vector" if l == 1 or (kind == "ln" and i == 0) else "pool"

        def bc3(ap, n):
            return ap.unsqueeze(1).broadcast_to([ap.shape[0], n, ap.shape[1]])

        block = ctx.enter_context(nc.Block())

        @block.sync
        def _(sp):
            sp.dma_start(Psb[:, 0:2, :], a["P"][0:256, :].rearrange("(s p) d -> p s d", p=128)).then_inc(p_in, 16)
            sp.dma_start(Psb[0:32, 2, :], a["P"][256:C, :]).then_inc(p_in, 16)
            sp.dma_start(T[:, :], a["P"][0:D, :]).then_inc(p_in, 16)
            sp.dma_start(PT[:, :], a["PT"]).then_inc(p_in, 16)
            sp.dma_start(bsk[:, :], a["bsk"]).then_inc(p_in, 16)
            sp.dma_start(ccol[:, :, :], a["cond"]).then_inc(p_in, 16)
            sp.dma_start(Wsk[:, 0:2, :], a["Wsk"][0:256, :].rearrange("(s p) n -> p s n", p=128)).then_inc(w_in, 16)
            sp.dma_start(Wsk[0:32, 2, :], a["Wsk"][256:C, :]).then_inc(w_in, 16)
            for b in range(B):
                sp.dma_start(X[:, TT * b:TT * b + TT, :], a["x"][b].rearrange("(t p) c -> p t c", p=128)).then_inc(x_in, 16)
            sp.dma_start(bacol[:, :, :, :], a["ada_bcol"]).then_inc(ada_b_in, 16)
            for l in range(LAYERS):
                sp.dma_start(barow[:, l, :, :], a["ada_brow"][l:l + 1].broadcast_to([B, 2, C])).then_inc(ada_b_in, 16)
                sp.dma_start(WA[:, l, 0:2, :], a["ada_w"][l, 0:256, :].rearrange("(s p) n -> p s n", p=128)).then_inc(ada_in[l], 16)
                sp.dma_start(WA[0:32, l, 2, :], a["ada_w"][l, 256:C, :]).then_inc(ada_in[l], 16)
            sp.wait_ge(ada_ev, 5 * LAYERS)
            for l in range(LAYERS):
                sp.dma_start(gate_rows[l], grow[:, l, :, :]).then_inc(gate_out, 16)
            sp.wait_ge(gate_out, 16 * LAYERS)
            phase_end(sp)

            def load3(dst, src, landed):
                sp.dma_start(dst[:, 0:2, :], src[0:256, :].rearrange("(s p) n -> p s n", p=128)).then_inc(landed, 16)
                for r in range(3):
                    sp.dma_start(dst[32 * r:32 * r + 32, 2, :], src[256:C, :]).then_inc(landed, 16)

            def wide(src):
                return src.broadcast_to([128, C])

            for l in range(LAYERS):
                phase_begin(sp, 2 * l + 1)
                load3(RawQ, a["w_qkv"][l], wq_in)
                sp.dma_start(WP[:, :, :], a["w_proj"][l]).then_inc(wp_in, 16)
                sp.dma_start(qkcol[:, :, :, :], a["qkcol"][l]).then_inc(wp_in, 16)
                sp.dma_start(vrow[:, :], wide(a["vrow"][l:l + 1])).then_inc(wp_in, 16)
                sp.dma_start(prow[:, :], wide(a["prow"][l:l + 1])).then_inc(wp_in, 16)
                for i in range(2):
                    sp.dma_start(qkrow[:, i, :], wide(a["qkrow"][l, i:i + 1])).then_inc(wp_in, 16)
                for b in range(B):
                    sp.dma_start(gbc[:, b, :], wide(gate_rows[l, b, 0:1, :])).then_inc(gate_in, 16)
                sp.wait_ge(att_zero, 2 * (l + 1))

                def place(b, j, which=(0, 1)):
                    if b > 0:
                        g = (START[j] + WIDTH[j] - 1) // 4
                        sp.wait_ge(b_full, 16 * (STEPS * l + 4 * (b - 1) + g + 1))
                    for qk in which:
                        dst = (Q3, K3)[qk]
                        for r, part in ((QR0, 0), (QR1, 1 - qk), (QR2, qk)):
                            sp.dma_start(
                                dst[r:r + HD, START[j]:START[j] + WIDTH[j], :].bitcast(F32),
                                stage[HD * j:HD * j + HD, qk, part, 0:WIDTH[j], :].bitcast(F32)).then_inc(qk_in[j], 16)

                def place_max(s):
                    sp.wait_ge(misc_free, MISC[l]["max", s, 0] + 1)
                    for i in range(4):
                        sp.dma_start(
                            Q3[QROW:QROW + 1, 4 * (s % 4) + i, :].bitcast(F32), Q3[96 + i:97 + i, 0, :].bitcast(F32)).then_inc(mrow_in, 16)

                sp.wait_ge(staged, 6 * 4 * l + 3)
                for j in range(2):
                    place(0, j, (0,))
                sp.wait_ge(staged, 6 * (4 * l + 1))
                for j in range(2):
                    place(0, j, (1,))
                for j in range(2, 7):
                    place(0, j)
                place_max(0)
                for s in range(STEPS):
                    b, g = divmod(s, 4)
                    if g == 0 and b > 0:
                        place(b, 5)
                        place(b, 6)
                    if s + 1 < STEPS:
                        place_max(s + 1)
                    if b + 1 < B:
                        if g == 1:
                            sp.wait_ge(staged, 6 * (4 * l + b + 2))
                            place(b + 1, 0)
                        if g == 2:
                            place(b + 1, 1)
                            place(b + 1, 2)
                        if g == 3:
                            place(b + 1, 3)
                            place(b + 1, 4)
                phase_end(sp)

                phase_begin(sp, 2 * l + 2)
                E = EXPERTS[l]
                for e in range(E):
                    for q in range(6):
                        n = 6 * (EBASE[l] + e) + q
                        if n >= 3:
                            sp.wait_ge(w_split, 2 * (n - 2))
                        if q < 2:
                            sp.dma_start(raw[:, n % 3, :], a[f"w1_{l}"][e, 128 * q:128 * q + 128, :]).then_inc(w_raw[n % 3], 16)
                        elif q == 2:
                            for r in range(3):
                                sp.dma_start(raw[32 * r:32 * r + 32, n % 3, :], a[f"w1_{l}"][e, 256:C, :]).then_inc(w_raw[n % 3], 16)
                        else:
                            k = 3 * (q - 3)
                            sp.dma_start(raw[:, n % 3, 0:3 * C].rearrange("p (t c) -> p t c", c=C),
                                 a[f"w2_{l}"][e, 128 * k:128 * (k + 3), :].rearrange("(t p) c -> p t c", p=128)).then_inc(w_raw[n % 3], 16)
                        if (e, q) != (0, 2):
                            continue
                        sp.dma_start(b1col[:, 0:E, :], a[f"b1_{l}"]).then_inc(wg_in, 16)
                        for i in range(E):
                            sp.dma_start(b2row[:, i, :], wide(a[f"b2_{l}"][i:i + 1])).then_inc(wg_in, 16)
                        for b in range(B):
                            sp.dma_start(gbc[:, b, :], wide(gate_rows[l, b, 1:2, :])).then_inc(wg_in, 16)
                        if E > 1:
                            load3(rawg, a["w_gate"], wg_in)
                phase_end(sp)
            phase_begin(sp, 2 * LAYERS + 1)
            for b in range(B):
                sp.dma_start(out[b].rearrange("(t p) c -> p t c", p=128), X[:, TT * b:TT * b + TT, :]).then_inc(out_done, 16)
            sp.wait_ge(out_done, 16 * B)

        def wg_in_total(l):
            n = 0
            for k in range(l + 1):
                n += 1 + EXPERTS[k] + B + (4 if EXPERTS[k] > 1 else 0)
            return 16 * n

        def raw_total(n):
            return 16 * ((2, 2, 4)[n % 3] * (n // 6) + (1, 1, 3, 2, 2, 4)[n % 6])

        @block.gpsimd
        def _(pool):
            pool.memset(ident[:, :], 0.0).then_inc(pool_done, 1)
            pool.wait_ge(pool_done, pool_step())
            pool.memset(ident2[:, :], 0.0).then_inc(pool_done, 1)
            pool.wait_ge(pool_done, pool_step())
            pool.memset(below[:, :], 0.0).then_inc(pool_done, 1)
            pool.wait_ge(pool_done, pool_step())
            pool.memset(neghalf[:, :], -0.5).then_inc(consts, 1)
            pool.memset(plushalf[:, :], 0.5).then_inc(consts, 1)
            pool.affine_select(out=ident[:, :], in_=ident[:, :], compare_op=ALU.not_equal, fill=1.0,
                               base=0, pattern=[[-1, 128]], channel_multiplier=1).then_inc(consts, 1)
            pool.affine_select(out=ident2[:, :], in_=ident2[:, :], compare_op=ALU.not_equal, fill=2.0,
                               base=0, pattern=[[-1, D]], channel_multiplier=1).then_inc(consts, 1)
            pool.affine_select(out=below[:, :], in_=below[:, :], compare_op=ALU.is_ge, fill=-1.0,
                               base=0, pattern=[[1, D]], channel_multiplier=-1).then_inc(consts, 1)
            pool.wait_ge(consts, 5)
            for j in range(D):
                pool.wait_ge(n2_ready, j + 1)
                pool.tensor_tensor(small[:, j % 2, 1:2], RG[:, j % 2, j:j + 1], plushalf[:, :], ALU.pow).then_inc(n2_root, 1)
            phase_end(pool)

            def norm_root(i):
                pool.wait_ge(var_ready, i + 1)
                pool.tensor_scalar(var4[:, :], mv[:, :, 1], LN_EPS, None, ALU.add).then_inc(pool_done, 1)
                pool.wait_ge(pool_done, pool_step())
                pool.tensor_tensor(rstd[:, :], var4[:, :], neghalf[:, 0:TT], ALU.pow).then_inc(rstd_ready, 1)
                pool.wait_ge(rstd_ready, i + 1)

            def heads_of(qk):
                return rowt[:, :, :] if qk else QN[:, :, :]

            def per_head(x):
                return x.unsqueeze(2).broadcast_to([128, x.shape[1], HD])

            def center(qk, b, t):
                n = 2 * TT * b + TT * qk + t
                x = heads_of(qk)[:, t, :]
                pool.wait_ge(qk_sum, n + 1)
                pool.tensor_scalar(qstat[:, 1, t, :], qstat[:, 0, t, :], 1.0 / HD, None, ALU.mult).then_inc(pool_done, 1)
                pool.wait_ge(pool_done, pool_step())
                xh = x.rearrange("p (h e) -> p h e", e=HD)
                pool.tensor_tensor(xh, xh, per_head(qstat[:, 1, t, :]), ALU.subtract).then_inc(pool_done, 1)
                pool.wait_ge(pool_done, pool_step())
                if n > 0:
                    pool.wait_ge(qk_var, n)
                pool.tensor_tensor(squares[:, :], x, x, ALU.mult).then_inc(qk_sq, 1)

            def head_roots(qk, b, t):
                n = 2 * TT * b + TT * qk + t
                v, r = qstat[:, 2, t, :], qstat[:, 3, t, :]
                pool.wait_ge(qk_var, n + 1)
                pool.tensor_scalar(v, v, 1.0 / HD, QK_EPS, ALU.mult, ALU.add).then_inc(pool_done, 1)
                pool.wait_ge(pool_done, pool_step())
                if b == 0:
                    pool.tensor_tensor(r, v, neghalf[:, :], ALU.pow).then_inc(qk_root, 1)
                    return
                pool.tensor_tensor(r, v, neghalf[:, :], ALU.pow).then_inc(pool_done, 1)
                pool.wait_ge(pool_done, pool_step())
                x = heads_of(qk)[:, t, :].rearrange("p (h e) -> p h e", e=HD)
                pool.tensor_tensor(x, x, per_head(r), ALU.mult).then_inc(qn_ready, 1)
                pool.wait_ge(qn_ready, n + 1)

            for l in range(LAYERS):
                phase_begin(pool, 2 * l + 1)
                if l == 0:
                    norm_root(8 * l)
                pool.memset(K3[0:64, :, :].bitcast(F32), 0.0).then_inc(pool_done, 1)
                pool.wait_ge(pool_done, pool_step())
                pool.memset(K3[64:96, :, :].bitcast(F32), 1.0).then_inc(pool_done, 1)
                pool.wait_ge(pool_done, pool_step())
                pool.memset(V[:, :, :, :], 1.0).then_inc(att_zero, 1)
                for kind, b, k in all_order(l):
                    if kind == "mean" and b > 0:
                        norm_root(8 * l + b)
                    if kind == "mean2":
                        norm_root(8 * l + 4)
                    if kind in ("ln", "q", "k") and low_engine(l, kind, b) == "pool":
                        pool.wait_ge(misc_free, MISC[l][kind, b, k] + 1)
                        low_of(pool, kind, b, k, HELD[l, "att", kind, b, k]).then_inc(act_split if kind == "ln" else staged, 1)
                        if kind == "ln":
                            pool.wait_ge(act_split, 3 * (4 * l + b) + k + 1)
                        else:
                            pool.wait_ge(staged, 6 * (4 * l + b) + 3 * "qk".index(kind) + k + 1)
                    if kind in ("qtok", "ktok") and b > 0:
                        center("qk".index(kind[0]), b, k)
                    if kind in ("qvar", "kvar"):
                        head_roots("qk".index(kind[0]), b, k)
                phase_end(pool)
                phase_begin(pool, 2 * l + 2)
                for b in range(B):
                    if b > 0:
                        norm_root(8 * l + 4 + b)
                    for c in range(3):
                        hi, lo, rows = parts(HM[:, b], c)
                        high = hi if c < 2 else HM[32:64, b, 4, :]
                        pool.wait_ge(norm_free, NORM[l]["ln", b, c] + 1)
                        pool.tensor_tensor(lo, act32[rows, HELD[l, "mlp", "ln", b, c] % 2, :], high.bitcast(F32),
                                           ALU.subtract).then_inc(hm_ready, 1)
                        pool.wait_ge(hm_ready, 3 * (4 * l + b) + c + 1)
                if l + 1 < LAYERS:
                    norm_root(8 * (l + 1))
                phase_end(pool)

        @block.vector
        def _(dve):
            for x in (GIz, Tz, BBz, EFz, PTz, YTz, Midz, YMz):
                flat = x[D:128]
                while len(flat.shape) > 2:
                    flat = flat.rearrange({3: "p a b -> p (a b)", 4: "p a b c -> p (a b) c", 5: "p a b c d -> p (a b) c d"}[len(flat.shape)])
                ins = dve.memset(flat, 0.0)
            ins.then_inc(pads, 1)
            dve.memset(ps[0:D, 6, 0:B * D], 0.0).then_inc(skew_zero, 1)
            dve.wait_ge(p_in, 96)
            dve.wait_ge(consts, 5)
            dve.wait_ge(silu_exp, 1)
            dve.tensor_scalar(cexp[:, :, :], cexp[:, :, :], 1.0, None, ALU.add).then_inc(dve_done, 1)
            dve.wait_ge(dve_done, step())
            dve.reciprocal(cexp[:, :, :], cexp[:, :, :]).then_inc(dve_done, 1)
            dve.wait_ge(dve_done, step())
            dve.tensor_tensor(csil[:, :, :], ccol[:, :, :], cexp[:, :, :], ALU.mult).then_inc(silu_done, 1)
            dve.tensor_copy(GI[:, D:2 * D], ident[0:D, 0:D])
            dve.wait_ge(gram, 1)
            dve.tensor_copy(GI[:, 0:D], ps[0:D, 0, 0:D]).then_inc(gi_upd, 1)
            dve.wait_ge(gi_upd, 1)

            def reduce_gram(j):
                k, r, m = j % 2, small[:, j % 2, 0:1], small[:, j % 2, 2:3]
                row = ps[0:D, k, 0:2 * D]
                dve.wait_ge(bc_g, j + 1)
                dve.reciprocal(r, row[:, j:j + 1]).then_inc(dve_done, 1)
                dve.wait_ge(dve_done, step())
                dve.scalar_tensor_tensor(out=m, in0=GI[:, j:j + 1], scalar=r, in1=below[:, j:j + 1],
                                         op0=ALU.mult, op1=ALU.mult).then_inc(dve_done, 1)
                dve.wait_ge(dve_done, step())
                dve.scalar_tensor_tensor(out=GI[:, :], in0=row, scalar=m, in1=GI[:, :],
                                         op0=ALU.mult, op1=ALU.add).then_inc(gi_upd, 1)
                dve.tensor_copy(RG[:, k, :], row[:, 0:D]).then_inc(n2_ready, 1)

            def reduce_top(j):
                k = j % 2
                n2, root = RG[:, k, j:j + 1], small[:, k, 1:2]
                sg, den, rd, m, nb = small[:, k, 3:4], small[:, k, 4:5], small[:, k, 5:6], small[:, k, 6:7], NB[:, j:j + 1]
                row = ps[0:D, 2 + k, 0:D]
                alpha = row[:, j:j + 1]
                dve.wait_ge(bc_t, j + 1)
                dve.tensor_scalar(sg, alpha, 0.0, 2.0, ALU.is_ge, ALU.mult).then_inc(dve_done, 1)
                dve.wait_ge(dve_done, step())
                dve.wait_ge(n2_root, j + 1)
                dve.wait_ge(n2_ready, j + 1)
                dve.tensor_scalar(nb, sg, -1.0, root, ALU.add, ALU.mult).then_inc(dve_done, 1)
                dve.wait_ge(dve_done, step())
                dve.tensor_scalar(den, alpha, nb, n2, ALU.mult, ALU.add).then_inc(dve_done, 1)
                dve.wait_ge(dve_done, step())
                dve.reciprocal(rd, den).then_inc(dve_done, 1)
                dve.wait_ge(dve_done, step())
                dve.scalar_tensor_tensor(out=m, in0=T[:, j:j + 1], scalar=rd, in1=below[:, j:j + 1],
                                         op0=ALU.mult, op1=ALU.mult)
                dve.scalar_tensor_tensor(out=RG[:, k, :], in0=row, scalar=nb, in1=RG[:, k, :],
                                         op0=ALU.mult, op1=ALU.add).then_inc(dve_done, 1)
                dve.wait_ge(dve_done, step())
                dve.scalar_tensor_tensor(out=T[:, :], in0=RG[:, k, :], scalar=m, in1=T[:, :],
                                         op0=ALU.mult, op1=ALU.add).then_inc(t_upd, 1)

            def skew_add():
                dve.wait_ge(skew_mm, 1)
                dve.tensor_tensor(Up[:, :, :], ps[0:D, 6, 0:B * D].rearrange("p (b j) -> p b j", b=B),
                                  bc3(bsk[:, :], B), ALU.add).then_inc(up_ready, 1)

            def skew_scale():
                dve.wait_ge(skew_t, 1)
                dve.wait_ge(up_ready, 1)
                dve.scalar_tensor_tensor(out=Up[:, :, :], in0=ps[0:D, 7, 0:B * D].rearrange("p (b j) -> p b j", b=B),
                                         scalar=-1.0, in1=Up[:, :, :], op0=ALU.mult, op1=ALU.add).then_inc(dve_done, 1)
                dve.wait_ge(dve_done, step())
                sc = 2.0 ** -SQUARINGS
                for i, x in enumerate((sc, -sc)):
                    dve.tensor_scalar(BB[:, i, :, :], Up[:, :, :], x, None, ALU.mult).then_inc(skew_done, 1)
                    dve.tensor_scalar(EF[:, 0, i, :, :], Up[:, :, :], x / DEGREE, None, ALU.mult).then_inc(skew_done, 1)

            def ada_add(l):
                dve.wait_ge(ada_mm, l + 1)
                dve.wait_ge(ada_b_in, 16 * (1 + LAYERS))
                n = 8 * B
                for rows, lo, hi in ((128, 0, 2), (96, 2, 3)):
                    dve.tensor_tensor(
                        ada[0:rows, l, lo:hi, :, :].rearrange("p c v b -> p (c v) b"),
                        ps[0:rows, 4, 4 * B * lo:4 * B * hi].rearrange("p (x b) -> p x b", b=B),
                        bacol[0:rows, l, lo:hi, :].rearrange("p c v -> p (c v)").unsqueeze(2).broadcast_to(
                            [rows, 4 * (hi - lo), B]), ALU.add).then_inc(ada_ev, 1)
                dve.wait_ge(ada_ev, 5 * l + 2)
                for rows, lo, hi in ((128, 0, 2), (96, 2, 3)):
                    for c in range(lo, hi):
                        x = ada[0:rows, l, c, 1::2, :]
                        ins = dve.tensor_scalar(x, x, 1.0, None, ALU.add)
                ins.then_inc(ada_ev, 1)
                for i, bank in ((0, 5), (1, 7)):
                    dve.tensor_tensor(grow[:, l, i, :], ps[0:B, bank, 0:C], barow[:, l, i, :], ALU.add).then_inc(ada_ev, 1)

            for j in range(D):
                reduce_gram(j)
                if j > 0:
                    reduce_top(j - 1)
                for at, kind, *args in BACKGROUND:
                    if kind == "turn" and j == at:
                        skew_add()
                    if kind == "turn" and j == at + 1:
                        skew_scale()
                    if kind == "ada" and args[1] == 9 and at == j - 1:
                        ada_add(args[0])
            reduce_top(D - 1)
            dve.wait_ge(t_upd, D)
            dve.wait_ge(gi_upd, D + 1)
            dve.tensor_tensor(NB[:, :], NB[:, :], ident[0:D, 0:D], ALU.mult).then_inc(dve_done, 1)
            dve.wait_ge(dve_done, step())
            dve.tensor_reduce(small[:, 0, 0:1], NB[:, :], AX, ALU.add, negate=True).then_inc(dve_done, 1)
            dve.wait_ge(dve_done, step())
            dve.reciprocal(small[:, 0, 1:2], small[:, 0, 0:1]).then_inc(dve_done, 1)
            dve.wait_ge(dve_done, step())
            dve.tensor_scalar(RT[:, :], GI[:, D:2 * D], small[:, 0, 1:2], None, ALU.mult).then_inc(rt_ready, 1)
            for b in range(B):
                for t in range(TT):
                    n = TT * b + t
                    dve.wait_ge(l0_mm, n + 1)
                    dve.tensor_tensor(X[:, n, :], X[:, n, :], ps[:, 4 + t, 0:C], ALU.add).then_inc(l0_done, 1)
            phase_end(dve)

            def norm_stats(b, t):
                dve.bn_stats(stats[:, t, :], X[:, TT * b + t, :]).then_inc(dve_done, 1)
                step()

            def norm_mean():
                dve.wait_ge(dve_done, steps[0])
                for t in range(TT):
                    dve.bn_aggr(mv[:, t, :], stats[:, t, :]).then_inc(dve_done, 1)
                    step()
                dve.wait_ge(dve_done, steps[0])
                dve.tensor_copy(rowt0[:, 0:TT], mv[:, :, 0]).then_inc(var_ready, 1)

            def norm_scale(i, b, tiles):
                dve.wait_ge(rstd_ready, i + 1)
                for t in tiles:
                    dve.tensor_scalar(xn[:, t, 0:C], X[:, TT * b + t, :], mv[:, t, 0:1], rstd[:, t:t + 1],
                                      ALU.subtract, ALU.mult).then_inc(dve_done, 1)
                    step()
                dve.wait_ge(dve_done, steps[0])
                for r in range(2):
                    dve.tensor_copy(xn[:, tiles[0]:tiles[-1] + 1, C + 32 * r:C + 32 * r + 32],
                                    xn[:, tiles[0]:tiles[-1] + 1, C - 32:C]).then_inc(xn_ready, 1)

            def norm(i, b, free):
                for t in range(TT):
                    norm_stats(b, t)
                norm_mean()
                free()
                norm_scale(i, b, (0, 1))
                norm_scale(i, b, (2, 3))

            def split_weights(dst, src, c):
                if c < 2:
                    dve.tensor_copy(dst[:, c, :], src[:, :]).then_inc(dve_done, 1)
                    dve.wait_ge(dve_done, step())
                    return dve.tensor_tensor(dst[:, 2 + c, :], src[:, :], dst[:, c, :].bitcast(F32), ALU.subtract)
                dve.tensor_copy(dst[0:96, 4, :], src[0:96, :]).then_inc(dve_done, 1)
                dve.wait_ge(dve_done, step())
                return dve.tensor_tensor(dst[64:96, 4, :], src[64:96, :], dst[64:96, 4, :].bitcast(F32), ALU.subtract)

            for l in range(LAYERS):
                M, W = MISC[l], NORM[l]
                phase_begin(dve, 2 * l + 1)


                def heads_of(qk):
                    return rowt[:, :, :] if qk else QN[:, :, :]

                def work(kind, i, k):
                    if kind == "max":
                        return
                    if kind == "stats":
                        norm_stats(i, k)
                        return
                    if kind == "mean":
                        norm_mean()
                        return
                    if kind == "scale":
                        if i > 0 and k == 0:
                            dve.wait_ge(misc_full, M["ln", i - 1, 2] + 1)
                        norm_scale(8 * l + i, i, (2 * k, 2 * k + 1))
                        return
                    if kind == "out":
                        if k == 0:
                            dve.wait_ge(av_done, 4 * (STEPS * l + i + 1))
                            if i > 0:
                                dve.wait_ge(ot_ready, STEPS * l + i)
                            dve.transpose(oTok[:, :, :].rearrange("p c e -> p (c e)"), ps[:, 6, :]).then_inc(o_out, 1)
                        elif k == 1:
                            dve.wait_ge(o_out, STEPS * l + i + 1)
                            dve.reciprocal(rsum[:, :], oTok[:, :, HD]).then_inc(o_rec, 1)
                        elif k == 2:
                            dve.wait_ge(o_rec, STEPS * l + i + 1)
                            dve.tensor_tensor(oTok[:, :, :], oTok[:, :, :],
                                              rsum[:, :].unsqueeze(2).broadcast_to([128, 16, 32]), ALU.mult).then_inc(o_mul, 1)
                        else:
                            dve.wait_ge(o_mul, STEPS * l + i + 1)
                            if i >= 5:
                                dve.wait_ge(misc_full, M["proj", (i - 5) // 4, TT - 1] + 1)
                            dve.transpose(oT[:, i % 5, :], oTok[:, :, :].rearrange("p c e -> p (c e)")).then_inc(ot_ready, 1)
                        return
                    if kind in ("qvar", "kvar"):
                        qk = "qk".index(kind[0])
                        v = 2 * TT * i + TT * qk + k
                        x = heads_of(qk)[:, k, :].rearrange("p (h e) -> p h e", e=HD)
                        sq = squares[:, :].rearrange("p (h e) -> p h e", e=HD)
                        if i == 0:
                            dve.wait_ge(qk_sum, v + 1)
                            dve.tensor_scalar(qstat[:, 1, k, :], qstat[:, 0, k, :], 1.0 / HD, None, ALU.mult).then_inc(dve_done, 1)
                            dve.wait_ge(dve_done, step())
                            dve.tensor_tensor(x, x, qstat[:, 1, k, :].unsqueeze(2).broadcast_to([128, H, HD]),
                                              ALU.subtract).then_inc(dve_done, 1)
                            dve.wait_ge(dve_done, step())
                            dve.tensor_tensor(sq, x, x, ALU.mult).then_inc(dve_done, 1)
                            dve.wait_ge(dve_done, step())
                        else:
                            dve.wait_ge(qk_sq, v - 2 * TT + 1)
                        if v >= TT:
                            dve.wait_ge(qn_ready, v - TT + 1)
                        dve.tensor_reduce(qstat[:, 2, k, :], sq, AX, ALU.add).then_inc(qk_var, 1)
                        if i == 0:
                            for w in ([v - 1] if k > 0 else []) + ([v] if k == TT - 1 else []):
                                dve.wait_ge(qk_root, w + 1)
                                y = heads_of(qk)[:, w % TT, :].rearrange("p (h e) -> p h e", e=HD)
                                dve.tensor_tensor(y, y, qstat[:, 3, w % TT, :].unsqueeze(2).broadcast_to([128, H, HD]),
                                                  ALU.mult).then_inc(qn_ready, 1)
                        return
                    if kind == "split":
                        dve.wait_ge(wq_in, 64 * (l + 1))
                        for c in range(3):
                            split_weights(WQ, RawQ[:, c, :], c).then_inc(wq_split, 1)
                        return
                    if kind == "zero":
                        dve.memset(Q3[0:96, :, :].bitcast(F32), 0.0).then_inc(att_zero, 1)
                        dve.wait_ge(wp_in, 96 * (l + 1))
                        dve.wait_ge(gate_in, 16 * B * (l + 1))
                        return
                    if kind == "stats2":
                        norm_stats(0, k)
                        return
                    if kind == "mean2":
                        norm_mean()
                        return
                    if kind == "scale2":
                        if k == 0:
                            dve.wait_ge(misc_full, M["ln", B - 1, 2] + 1)
                        norm_scale(8 * l + 4, 0, (2 * k, 2 * k + 1))
                        return
                    n = M[kind, i, k]
                    if kind in ("ln", "q", "k"):
                        if low_engine(l, kind, i) == "vector":
                            dve.wait_ge(misc_free, n + 1)
                            low_of(dve, kind, i, k, HELD[l, "att", kind, i, k]).then_inc(act_split if kind == "ln" else staged, 1)
                        return
                    dve.wait_ge(misc_full, n + 1)
                    bank = ps[:, shared(l, (kind, i, k)), :]
                    if kind == "v":
                        if k == 0:
                            if i == 0:
                                dve.wait_ge(att_zero, 2 * (l + 1))
                            if i >= 2:
                                dve.wait_ge(av_done, 4 * (STEPS * l + 4 * (i - 1)))
                        dve.tensor_tensor(
                            V[:, i % 2, k, 0:H * VW].rearrange("p (h e) -> p h e", e=VW)[:, :, 0:HD],
                            bank[:, 0:C].rearrange("p (h e) -> p h e", e=HD),
                            vrow[:, :].rearrange("p (h e) -> p h e", e=HD), ALU.add).then_inc(misc_free, 1)
                    elif kind == "proj":
                        x = ptmp[:, :]
                        dve.wait_ge(dve_done, steps[0])
                        dve.tensor_tensor(x, bank[:, 0:C], prow[:, :], ALU.add).then_inc(misc_free, 1)
                        dve.wait_ge(misc_free, n + 1)
                        dve.tensor_tensor(x, x, gbc[:, i, :], ALU.mult).then_inc(dve_done, 1)
                        dve.wait_ge(dve_done, step())
                        dve.tensor_tensor(X[:, TT * i + k, :], X[:, TT * i + k, :], x, ALU.add).then_inc(dve_done, 1)
                        step()
                    elif kind in ("qtok", "ktok"):
                        qk = "qk".index(kind[0])
                        t = heads_of(qk)[:, k, :]
                        if k == 0 and i > 0:
                            dve.wait_ge(misc_full, M["qk"[qk], i - 1, NM - 1] + 1)
                        dve.tensor_tensor(t, bank[:, 0:C], qkrow[:, qk, :], ALU.add).then_inc(misc_free, 1)
                        dve.wait_ge(misc_free, n + 1)
                        dve.tensor_reduce(qstat[:, 0, k, :], t.rearrange("p (h e) -> p h e", e=HD),
                                          AX, ALU.add).then_inc(qk_sum, 1)

                def negmax_unit(s, i):
                    n = 16 * (STEPS * l + s) + i
                    if i == 0 and s >= 2:
                        dve.wait_ge(misc_full, M["max", s - 2, 0] + 1)
                    dve.wait_ge(a_full, n + 1)
                    dve.tensor_reduce(negmax[:, s % 2, i % 4, i // 4:i // 4 + 1], ps[:, 3 + n % 3, :],
                                      AX, ALU.max, negate=True).then_inc(a_free, 1)

                for key in prologue(l):
                    work(*key)
                for i in range(32):
                    for at, *key in warm_up(l):
                        if at == i:
                            work(*key)
                    negmax_unit(i // 16, i % 16)
                for s in range(STEPS):
                    for u in range(9):
                        for at, *key in plan(l, s):
                            if u == (at + 1 if key[0] in ("ln", "q", "k") else at):
                                work(*key)
                        if s + 2 < STEPS and u < 8:
                            negmax_unit(s + 2, 2 * u)
                            negmax_unit(s + 2, 2 * u + 1)
                for key in EPILOGUE:
                    work(*key)
                dve.wait_ge(dve_done, steps[0])
                phase_end(dve)

                phase_begin(dve, 2 * l + 2)
                E = EXPERTS[l]

                def mlp_norm(b):
                    def free():
                        dve.wait_ge(norm_full, W["ln", b - 1, 2] + 1)
                    norm(8 * l + 4 + b, b, free)

                def piece(e, q):
                    n = 6 * (EBASE[l] + e) + q
                    k = (EBASE[l] + e) % 2
                    dve.wait_ge(w_raw[n % 3], raw_total(n))
                    src = raw[:, n % 3, :]
                    if e > 0:
                        dve.wait_ge(acc_full, 4 * B * (EBASE[l] + e - 1)) if e > 1 or l > 0 else None
                    if q < 3:
                        if q < 2:
                            hi, lo, s_ = W1[:, k, q, :], W1[:, k, 2 + q, :], src
                            dve.tensor_copy(hi, s_).then_inc(w_split, 1)
                            dve.wait_ge(w_split, 2 * n + 1)
                            dve.tensor_tensor(lo, s_, hi.bitcast(F32), ALU.subtract).then_inc(w_split, 1)
                        else:
                            dve.tensor_copy(W1[0:96, k, 4, :], src[0:96, :]).then_inc(w_split, 1)
                            dve.wait_ge(w_split, 2 * n + 1)
                            dve.tensor_tensor(W1[64:96, k, 4, :], src[64:96, :],
                                              W1[64:96, k, 4, :].bitcast(F32), ALU.subtract).then_inc(w_split, 1)
                    else:
                        j = 3 * (q - 3)
                        s_ = src[:, 0:3 * C].rearrange("p (t c) -> p t c", c=C)
                        dve.tensor_copy(W2[:, k, 0, j:j + 3, :], s_).then_inc(w_split, 1)
                        dve.wait_ge(w_split, 2 * n + 1)
                        dve.tensor_tensor(W2[:, k, 1, j:j + 3, :], s_,
                                          W2[:, k, 0, j:j + 3, :].bitcast(F32), ALU.subtract).then_inc(w_split, 1)

                def split_hidden(n):
                    dve.wait_ge(f_free, n + 1)
                    if n >= 3:
                        U, ft = divmod(n - 3, FT)
                        if ft < FT - 1:
                            dve.wait_ge(g_used, (FT - 1) * U + ft + 1)
                        else:
                            dve.wait_ge(acc_full, TT * (U + 1))
                    x, k = g32[:, n % 2, :], n % 3
                    dve.tensor_copy(G[:, k, 0, :], x).then_inc(g_ready, 1)
                    dve.wait_ge(g_ready, 2 * n + 1)
                    dve.tensor_tensor(G[:, k, 1, :], x, G[:, k, 0, :].bitcast(F32), ALU.subtract).then_inc(g_ready, 1)

                def finish(U, e, b):
                    for t in range(TT):
                        dve.wait_ge(acc_full, TT * U + t + 1)
                        dve.tensor_tensor(rowt[:, t, :], ps[:, t, 0:C], b2row[:, e, :], ALU.add).then_inc(acc_free, 1)
                    dve.wait_ge(acc_free, TT * (U + 1))
                    dve.tensor_tensor(rowt[:, :, :], rowt[:, :, :], bc3(gbc[:, b, :], TT), ALU.mult).then_inc(dve_done, 1)
                    dve.wait_ge(dve_done, step())
                    xs = X[:, TT * b:TT * b + TT, :]
                    if E == 1:
                        dve.tensor_tensor(xs, xs, rowt[:, :, :], ALU.add).then_inc(dve_done, 1)
                        dve.wait_ge(dve_done, step())
                    else:
                        for t in range(TT):
                            dve.scalar_tensor_tensor(out=X[:, TT * b + t, :], in0=rowt[:, t, :],
                                                     scalar=cw[:, b, t, e:e + 1], in1=X[:, TT * b + t, :],
                                                                  op0=ALU.mult, op1=ALU.add).then_inc(dve_done, 1)
                            step()
                        dve.wait_ge(dve_done, steps[0])

                def choose(b):
                    dve.wait_ge(norm_full, W["gate", b, 0] + 1)
                    dve.tensor_copy(lg[:, :, :], ps[:, 7, 0:4 * TT].rearrange("p (t e) -> p t e", e=4)).then_inc(norm_free, 1)
                    dve.wait_ge(norm_free, W["gate", b, 0] + 1)
                    dve.tensor_reduce(top[:, 0, :], lg[:, :, :], AX, ALU.max).then_inc(dve_done, 1)
                    dve.wait_ge(dve_done, step())
                    dve.tensor_tensor(tmp4[:, 0, :, :], lg[:, :, :],
                                      top[:, 0, :].unsqueeze(2).broadcast_to([128, TT, 4]), ALU.subtract).then_inc(logits, 1)
                    pairs = ((0, 1), (0, 2), (0, 3), (1, 2), (1, 3), (2, 3))
                    for p, (i, j) in enumerate(pairs):
                        dve.tensor_tensor(wins[:, :, p:p + 1], lg[:, :, i:i + 1], lg[:, :, j:j + 1], ALU.is_ge).then_inc(dve_done, 1)
                        step()
                    dve.wait_ge(dve_done, steps[0])

                    def w(i, j):
                        p = pairs.index((i, j))
                        return wins[:, :, p:p + 1]

                    c = [chosen[:, :, e:e + 1] for e in range(4)]
                    dve.tensor_tensor(c[0], w(0, 1), w(0, 2), ALU.add).then_inc(dve_done, 1)
                    step()
                    dve.tensor_tensor(c[1], w(0, 1), w(1, 2), ALU.subtract).then_inc(dve_done, 1)
                    step()
                    dve.tensor_tensor(c[2], w(0, 2), w(1, 2), ALU.add).then_inc(dve_done, 1)
                    step()
                    dve.tensor_tensor(c[3], w(0, 3), w(1, 3), ALU.add).then_inc(dve_done, 1)
                    step()
                    dve.wait_ge(dve_done, steps[0])
                    dve.tensor_tensor(c[0], c[0], w(0, 3), ALU.add).then_inc(dve_done, 1)
                    step()
                    dve.tensor_tensor(c[1], c[1], w(1, 3), ALU.subtract).then_inc(dve_done, 1)
                    step()
                    dve.tensor_tensor(c[2], c[2], w(2, 3), ALU.subtract).then_inc(dve_done, 1)
                    step()
                    dve.tensor_tensor(c[3], c[3], w(2, 3), ALU.add).then_inc(dve_done, 1)
                    step()
                    dve.wait_ge(dve_done, steps[0])
                    for e, (op, x) in enumerate(((ALU.is_ge, 2.0), (ALU.is_lt, 0.0), (ALU.is_lt, 1.0), (ALU.is_lt, 2.0))):
                        dve.tensor_scalar(c[e], c[e], x, None, op).then_inc(dve_done, 1)
                        step()
                    dve.wait_ge(dve_done, steps[0])

                def weigh(b):
                    dve.wait_ge(cw_exp, b + 1)
                    dve.tensor_tensor(tmp4[:, 1, :, :], tmp4[:, 1, :, :], chosen[:, :, :], ALU.mult).then_inc(dve_done, 1)
                    dve.wait_ge(dve_done, step())
                    dve.tensor_reduce(top[:, 0, :], tmp4[:, 1, :, :], AX, ALU.add).then_inc(dve_done, 1)
                    dve.wait_ge(dve_done, step())
                    dve.reciprocal(top[:, 1, :], top[:, 0, :]).then_inc(dve_done, 1)
                    dve.wait_ge(dve_done, step())
                    dve.tensor_tensor(cw[:, b, :, :], tmp4[:, 1, :, :],
                                      top[:, 1, :].unsqueeze(2).broadcast_to([128, TT, 4]), ALU.mult).then_inc(dve_done, 1)
                    dve.wait_ge(dve_done, step())

                for q in range(3):
                    piece(0, q)
                for q in range(3, 6):
                    piece(0, q)
                dve.wait_ge(wg_in, wg_in_total(l))
                if E > 1:
                    for c in range(3):
                        split_weights(Wg, rawg[:, c, :], c).then_inc(wg_split, 1)
                units = [(e, b) for e in range(E) for b in range(B)]
                for v, (e, b) in enumerate(units):
                    U = B * EBASE[l] + v
                    for ft in range(FT):
                        if e == 0:
                            if ft == 4 and b + 1 < B:
                                mlp_norm(b + 1)
                            for kind, i, c in norm_plan(l, b, ft):
                                if kind == "gate":
                                    choose(i)
                            if E > 1 and ft == 3:
                                weigh(b)
                        if v == len(units) - 1 and ft == 5 and l + 1 < LAYERS:
                            norm(8 * (l + 1), 0, lambda: dve.wait_ge(norm_full, W["ln", B - 1, 2] + 1))
                        split_hidden(FT * U + ft)
                        if ft == 1 and v > 0:
                            finish(U - 1, *units[v - 1])
                        if e + 1 < E and b > 0 and ft in (3, 6):
                            piece(e + 1, 2 * (b - 1) + (ft == 6))
                finish(B * EBASE[l] + len(units) - 1, *units[-1])
                phase_end(dve)

        @block.scalar
        def _(act):
            act.wait_ge(p_in, 96)
            act.activation(cexp[:, :, :], ccol[:, :, :], ACT.Exp, scale=-1.0).then_inc(silu_exp, 1)

            def xt_copy(b, c):
                n = 3 * b + c
                rows = 128 if c < 2 else 32
                act.wait_ge(xt_mm, n + 1)
                if b > 0:
                    act.wait_ge(y_mm, b)
                act.activation(XT[0:rows, c, :], ps[0:rows, 4, :], ACT.Copy).then_inc(xt_ev, 1)

            def y_copy(b):
                act.wait_ge(y_mm, b + 1)
                act.activation(YT[:, b, :], ps[0:D, 5, :], ACT.Copy).then_inc(y_ev, 1)

            def exp_copy(r):
                act.wait_ge(exp_mm, 2 * r + 2)
                k = 1.0 / (DEGREE - 1 - r) if r < DEGREE - 1 else 1.0
                act.activation(EF[:, (r + 1) % 2].rearrange("p x b j -> p (x b j)"), ps[0:D, 6, :],
                               ACT.Copy, scale=k).then_inc(exp_ev, 1)

            for at, kind, *args in BACKGROUND:
                if kind == "x":
                    xt_copy(*args)
                if kind == "y":
                    y_copy(*args)
                if kind == "exp" and args[1] == 1:
                    exp_copy(args[0])
            act.wait_ge(mid_mm, 1)
            act.activation(X1[:, :, :].rearrange("p b j -> p (b j)"), ps[0:D, 0, 0:B * D], ACT.Copy).then_inc(mid_ev, 1)
            act.wait_ge(mid_mm, 2)
            act.activation(Mid[:, :, :].rearrange("p b j -> p (b j)"), ps[0:D, 1, 0:B * D], ACT.Copy).then_inc(mid_ev, 1)
            for b in range(B):
                act.wait_ge(ym_mm, b + 1)
                if b >= 2:
                    act.wait_ge(l0_mm, TT * (b - 1))
                act.activation(YM[:, b % 2, :], ps[0:D, 2 + b % 2, :], ACT.Copy).then_inc(ym_ev, 1)
            phase_end(act)

            def hold(where, l, key):
                h = HELD[(l, where, *key)]
                if h >= 2:
                    pl, pw, *pk = held[h - 2]
                    if pw == "mlp":
                        act.wait_ge(hm_ready, 3 * (4 * pl + pk[1]) + pk[2] + 1)
                    elif pk[0] == "ln":
                        act.wait_ge(act_split, 3 * (4 * pl + pk[1]) + pk[2] + 1)
                    else:
                        act.wait_ge(staged, 6 * (4 * pl + pk[1]) + 3 * "qk".index(pk[0]) + pk[2] + 1)
                return act32[:, h % 2, :]

            for l in range(LAYERS):
                M, W = MISC[l], NORM[l]
                phase_begin(act, 2 * l + 1)

                def work(kind, i, k):
                    n = M[kind, i, k]
                    if kind == "max":
                        act.wait_ge(misc_full, n + 1)
                        if STEPS * l + i > 0:
                            act.wait_ge(mrow_in, 64 * (STEPS * l + i))
                        act.activation(mrow, ps[0:4, 7, :], ACT.Copy).then_inc(misc_free, 1)
                    elif kind == "ln":
                        act.wait_ge(misc_full, n + 1)
                        rows = 128 if k < 2 else 96
                        if k == 0 and i > 0:
                            act.wait_ge(misc_full, M["v", i - 1, TT - 1] + 1)
                        shift, scale = ada[0:rows, l, k, 0, i:i + 1], ada[0:rows, l, k, 1, i:i + 1]
                        dst = hold("att", l, (kind, i, k))
                        act.activation(dst[0:rows, :], ps[0:rows, shared(l, (kind, i, k)), :], ACT.Identity, bias=shift, scale=scale)
                        act.activation(parts(HQ, k)[0], ps[0:rows, shared(l, (kind, i, k)), :], ACT.Identity,
                                       bias=shift, scale=scale).then_inc(misc_free, 1)
                    elif kind in ("q", "k"):
                        act.wait_ge(misc_full, n + 1)
                        rows, qk = MROWS[k], "qk".index(kind)
                        if kind == "q" and k == 0 and i > 0:
                            for placed in qk_in:
                                act.wait_ge(placed, 96 * (4 * l + i))
                        if kind == "q" and k == 0 and i == 0:
                            act.wait_ge(wp_in, 96 * (l + 1))
                        dst = hold("att", l, (kind, i, k))
                        bias, scale = qkcol[0:rows, qk, k, 1:2], qkcol[0:rows, qk, k, 0:1] if l == 1 else 1.0
                        act.activation(dst[0:rows, :], ps[0:rows, shared(l, (kind, i, k)), :], ACT.Identity, bias=bias, scale=scale)
                        act.activation(stage[0:rows, qk, 0, k, :], ps[0:rows, shared(l, (kind, i, k)), :], ACT.Identity,
                                       bias=bias, scale=scale).then_inc(misc_free, 1)

                def exp_unit(s, u):
                    n, v = 16 * (STEPS * l + s) + u, 4 * (STEPS * l + s) + u // 4
                    if n == 16 * STEPS * l:
                        act.wait_ge(wq_split, 3 * (l + 1))
                    act.wait_ge(b_full, n + 1)
                    if u % 4 == 0 and v >= 2:
                        act.wait_ge(av_done, v - 1)
                    act.activation(Pr[:, (u // 4) % 2, u % 4, :], ps[:, n % 3, :], ACT.Exp, scale=SCALE).then_inc(b_free, 1)

                for key in prologue(l) + [x[1:] for x in warm_up(l)]:
                    if key[0] in BANK:
                        work(*key)
                for s in range(STEPS):
                    for u in range(8):
                        for at, *key in plan(l, s):
                            if at == u and key[0] in BANK:
                                work(*key)
                        exp_unit(s, 2 * u)
                        exp_unit(s, 2 * u + 1)
                phase_end(act)

                phase_begin(act, 2 * l + 2)
                E = EXPERTS[l]
                gelu = ACT.Gelu if l == 1 else ACT.Gelu_apprx_tanh

                def take_norm(b, c):
                    rows = 128 if c < 2 else 96
                    act.wait_ge(norm_full, W["ln", b, c] + 1)
                    dst = hold("mlp", l, ("ln", b, c))
                    shift, scale = ada[0:rows, l, c, 2, b:b + 1], ada[0:rows, l, c, 3, b:b + 1]
                    act.activation(dst[0:rows, :], ps[0:rows, 7, :], ACT.Identity, bias=shift, scale=scale)
                    act.activation(parts(HM[:, b], c)[0], ps[0:rows, 7, :], ACT.Identity,
                                   bias=shift, scale=scale).then_inc(norm_free, 1)

                for c in range(3):
                    take_norm(0, c)
                act.wait_ge(wg_in, wg_in_total(l))
                for v in range(E * B):
                    e, b = divmod(v, B)
                    for ft in range(FT):
                        n = FT * (B * EBASE[l] + v) + ft
                        if e == 0:
                            for kind, i, c in norm_plan(l, b, ft):
                                if kind == "ln":
                                    take_norm(i, c)
                            if E > 1 and ft == 2:
                                act.wait_ge(logits, b + 1)
                                act.activation(tmp4[:, 1, :, :], tmp4[:, 0, :, :], ACT.Exp).then_inc(cw_exp, 1)
                        act.wait_ge(f_full, n + 1)
                        if n >= 2:
                            act.wait_ge(g_ready, 2 * (n - 1))
                        act.activation(g32[:, n % 2, :], ps[:, 4 + n % 3, :], gelu,
                                       bias=b1col[:, e, ft:ft + 1]).then_inc(f_free, 1)
                phase_end(act)

        @block.tensor
        def _(pe):
            mm = pe.matmul
            KD = (128, 128, 32)

            pe.wait_ge(p_in, 96)
            for c in range(3):
                ins = mm(ps[0:D, 0, 0:D], Psb[0:KD[c], c, :], Psb[0:KD[c], c, :], start=c == 0, stop=c == 2)
            ins.then_inc(gram, 1)
            pe.wait_ge(consts, 5)
            pe.wait_ge(pads, 1)

            def spread_gram(j):
                pe.wait_ge(gi_upd, j + 1)
                if j >= 2:
                    pe.wait_ge(n2_ready, j - 1)
                k = j % 2
                mm(ps[0:D, k, 0:2 * D], ident[:, j:j + 1].broadcast_to([128, D]), GIz[:, :],
                   start=True, stop=True).then_inc(bc_g, 1)

            def spread_top(j):
                if j > 0:
                    pe.wait_ge(t_upd, j)
                k = j % 2
                mm(ps[0:D, 2 + k, 0:D], ident[:, j:j + 1].broadcast_to([128, D]), Tz[:, :],
                   start=True, stop=True).then_inc(bc_t, 1)

            def x_transpose(b, c):
                n = 3 * b + c
                pe.wait_ge(x_in, 16 * B)
                if n > 0:
                    pe.wait_ge(xt_ev, n)
                for t in range(TT):
                    ins = pe.transpose(ps[0:KD[c], 4, 128 * t:128 * t + 128], X[:, TT * b + t, 128 * c:128 * c + KD[c]],
                                       ident[:, :])
                ins.then_inc(xt_mm, 1)

            def y_product(b):
                pe.wait_ge(xt_ev, 3 * b + 3)
                if b > 0:
                    pe.wait_ge(y_ev, b)
                for c in range(3):
                    ins = mm(ps[0:D, 5, :], Psb[0:KD[c], c, :], XT[0:KD[c], c, :], start=c == 0, stop=c == 2)
                ins.then_inc(y_mm, 1)

            def skew_columns(j0, j1):
                pe.wait_ge(w_in, 32)
                pe.wait_ge(silu_done, 1)
                pe.wait_ge(skew_zero, 1)
                o = ps[0:D, 6, 0:B * D].rearrange("p (b j) -> p b j", b=B)
                for j in range(j0, j1):
                    at = j * (j - 1) // 2
                    for c in range(3):
                        ins = mm(o[0:j, :, j], Wsk[0:KD[c], c, at:at + j], csil[0:KD[c], c, :], start=c == 0, stop=c == 2)
                if j1 == D:
                    ins.then_inc(skew_mm, 1)

            def skew_transpose():
                pe.wait_ge(up_ready, 1)
                for b in range(B):
                    ins = pe.transpose(ps[0:D, 7, D * b:D * b + D], Up[:, b, :], ident[0:D, 0:D])
                ins.then_inc(skew_t, 1)

            def exp_half(r, x):
                if r == 0:
                    pe.wait_ge(skew_done, 4)
                else:
                    pe.wait_ge(exp_ev, r)
                cur = EFz[:, r % 2]
                for b in range(B):
                    at = 256 * x + D * b
                    left = BBz[:, 1 - x, b, :] if r < DEGREE - 1 else cur[:, 1 - x, b, :]
                    one = ident[:, 0:D] if r < DEGREE - 1 else ident2[:, :]
                    o = ps[0:D, 6, at:at + D]
                    mm(o, left, cur[:, x, b, :], start=True, stop=False)
                    ins = mm(o, left, one, start=False, stop=True)
                ins.then_inc(exp_mm, 1)

            def ada_products(l, piece):
                if piece == 0:
                    pe.wait_ge(ada_in[l], 32)
                    pe.wait_ge(silu_done, 1)
                    pe.wait_ge(y_ev, B)
                    pe.wait_ge(skew_done, 4)
                    if l > 0:
                        pe.wait_ge(ada_ev, 5 * l)
                if piece < 8:
                    vec = (0, 1, 3, 4)
                    c = min(piece // 2, 2)
                    for v in ((2 * piece) % 4, (2 * piece) % 4 + 1) if c < 2 else (piece - 4,):
                        for r in range(1 if c < 2 else 3):
                            rows = 128 if c < 2 else 32
                            at = C * vec[v] + 128 * c
                            for k in range(3):
                                mm(ps[32 * r:32 * r + rows, 4, B * (4 * c + v):B * (4 * c + v) + B],
                                   WA[0:KD[k], l, k, at:at + rows], csil[0:KD[k], k, :], start=k == 0, stop=k == 2)
                    return
                i = piece - 8
                for k in range(3):
                    ins = mm(ps[0:B, (5, 7)[i], 0:C], csil[0:KD[k], k, :], WA[0:KD[k], l, k, C * (2 + 3 * i):C * (3 + 3 * i)],
                             start=k == 0, stop=k == 2)
                if i == 1:
                    ins.then_inc(ada_mm, 1)

            background = dict(x=x_transpose, y=y_product, skew=skew_columns, turn=lambda: skew_transpose(), exp=exp_half,
                              ada=ada_products)
            spread_gram(0)
            for j in range(D):
                if j + 1 < D:
                    spread_gram(j + 1)
                for at, kind, *args in BACKGROUND:
                    if at == j:
                        background[kind](*args)
                spread_top(j)
            for at, kind, *args in BACKGROUND:
                if at >= D:
                    background[kind](*args)
            pe.wait_ge(rt_ready, 1)
            pe.wait_ge(exp_ev, ROUNDS)
            for b in range(B):
                ins = mm(ps[0:D, 0, D * b:D * b + D], EF[:, ROUNDS % 2, 1, b, :], RT[:, :], start=True, stop=True)
            ins.then_inc(mid_mm, 1)
            pe.wait_ge(mid_ev, 1)
            mm(ps[0:D, 1, 0:B * D], RT[:, :], X1[:, :, :].rearrange("p b j -> p (b j)"), start=True, stop=True).then_inc(mid_mm, 1)
            pe.wait_ge(mid_ev, 2)
            pe.wait_ge(ada_ev, 5 * LAYERS)
            for b in range(B + 1):
                if b < B:
                    if b >= 2:
                        pe.wait_ge(ym_ev, b - 1)
                    mm(ps[0:D, 2 + b % 2, :], Midz[:, b, :], YTz[:, b, :], start=True, stop=True).then_inc(ym_mm, 1)
                if b > 0:
                    pe.wait_ge(ym_ev, b)
                    for t in range(TT):
                        n = TT * (b - 1) + t
                        if n >= TT:
                            pe.wait_ge(l0_done, n - TT + 1)
                        mm(ps[:, 4 + t, 0:C], YMz[:, (b - 1) % 2, 128 * t:128 * t + 128], PTz[:, :],
                           start=True, stop=True).then_inc(l0_mm, 1)
            phase_end(pe)

            def seven(o, lhs, rhs):
                for p in range(7):
                    w, h = PASSES[p]
                    ins = mm(o, lhs(w, h, KROWS[w]), rhs(w, h, KROWS[w]), start=p == 0, stop=p == 6)
                return ins

            for l in range(LAYERS):
                M, W = MISC[l], NORM[l]
                phase_begin(pe, 2 * l + 1)

                def work(kind, i, k):
                    n = M[kind, i, k]
                    if n > 0:
                        pe.wait_ge(misc_free, n - 1 if two_banks(l, (kind, i, k)) else n)
                    bank = ps[:, shared(l, (kind, i, k)), :]
                    if kind == "ln":
                        pe.wait_ge(xn_ready, 4 * (8 * l + i + 1))
                        rows = 128 if k < 2 else 96
                        for t in range(TT):
                            ins = pe.transpose(bank[0:rows, 128 * t:128 * t + 128], xn[:, t, 128 * k:128 * k + rows], ident[:, :])
                    elif kind in ("q", "k") and l == 1:
                        qk = "qk".index(kind)
                        pe.wait_ge(qn_ready, 2 * TT * i + TT * (qk + 1))
                        src = rowt if qk else QN
                        for t in range(TT):
                            ins = pe.transpose(bank[0:MROWS[k], 128 * t:128 * t + 128], src[:, t, 126 * k:126 * k + MROWS[k]],
                                               ident[:, :])
                    elif kind in ("q", "k"):
                        pe.wait_ge(act_split, 3 * (4 * l + i) + 3)
                        pe.wait_ge(wq_split, 3 * (l + 1))
                        at = C * "qk".index(kind) + 126 * k
                        ins = seven(bank[0:MROWS[k], :], lambda w, h, r: WQ[0:r, w, at:at + MROWS[k]],
                                    lambda w, h, r: HQ[0:r, h, :])
                    elif kind in ("v", "qtok", "ktok"):
                        pe.wait_ge(act_split, 3 * (4 * l + i) + 3)
                        pe.wait_ge(wq_split, 3 * (l + 1))
                        at = C * "qkv".index(kind[0])
                        ins = seven(bank[:, 0:C], lambda w, h, r: HQ[0:r, h, 128 * k:128 * k + 128],
                                    lambda w, h, r: WQ[0:r, w, at:at + C])
                    elif kind == "max":
                        pe.wait_ge(a_free, 16 * (STEPS * l + i + 1))
                        for t in range(TT):
                            ins = pe.transpose(bank[0:4, 128 * t:128 * t + 128], negmax[:, i % 2, t, :], ident[:, :])
                    elif kind == "proj":
                        pe.wait_ge(wp_in, 96 * (l + 1))
                        pe.wait_ge(ot_ready, STEPS * l + 4 * i + 4)
                        for g in range(4):
                            ins = mm(bank[:, 0:C], oT[:, (4 * i + g) % 5, 128 * k:128 * k + 128], WP[:, g, :],
                                     start=g == 0, stop=g == 3)
                    ins.then_inc(misc_full, 1)

                def query_scores(s, i):
                    n = 16 * (STEPS * l + s) + i
                    h = 4 * (s % 4) + i // 4
                    if i % 4 == 0:
                        pe.wait_ge(qk_in[POSITION[h]], 96 * (4 * l + s // 4 + 1))
                    if n >= 3:
                        pe.wait_ge(a_free, n - 2)
                    t = i % 4
                    mm(ps[:, 3 + n % 3, :], Q3[0:QK_ROWS, h, 128 * t:128 * t + 128], K3[0:QK_ROWS, h, :],
                       start=True, stop=True).then_inc(a_full, 1)

                def key_scores(s, u):
                    n = 16 * (STEPS * l + s) + u
                    if u == 0:
                        pe.wait_ge(mrow_in, 64 * (STEPS * l + s + 1))
                    if n >= 3:
                        pe.wait_ge(b_free, n - 2)
                    h, t = 4 * (s % 4) + u % 4, u // 4
                    mm(ps[:, n % 3, :], K3[0:QROW + 1, h, 128 * t:128 * t + 128], Q3[0:QROW + 1, h, :],
                       start=True, stop=True).then_inc(b_full, 1)

                def values(s, t):
                    n = STEPS * l + s
                    pe.wait_ge(b_free, 16 * n + 4 * t + 4)
                    if t == 0:
                        pe.wait_ge(misc_free, M["v", s // 4, TT - 1] + 1)
                        if n > 0:
                            pe.wait_ge(o_out, n)
                    for i in range(4):
                        at = VW * (4 * (s % 4) + i)
                        ins = mm(ps[32 * i:32 * i + 32, 6, :], V[:, s // 4 % 2, t, at:at + 32], Pr[:, t % 2, i, :],
                                 start=t == 0, stop=t == TT - 1)
                    ins.then_inc(av_done, 1)

                for key in prologue(l):
                    if key[0] in BANK:
                        work(*key)
                for i in range(32):
                    for at, *key in warm_up(l):
                        if at == i and key[0] in BANK:
                            work(*key)
                    query_scores(i // 16, i % 16)
                for s in range(STEPS):
                    for u in range(8):
                        for at, *key in plan(l, s):
                            if at == u and key[0] in BANK:
                                work(*key)
                        for i in (2 * u, 2 * u + 1):
                            key_scores(s, i)
                            if s + 2 < STEPS:
                                query_scores(s + 2, i)
                        if u == 0 and s > 0:
                            values(s - 1, TT - 1)
                        if u in (2, 4, 6):
                            values(s, (u - 2) // 2)
                values(STEPS - 1, TT - 1)
                for key in EPILOGUE:
                    if key[0] in BANK:
                        work(*key)
                phase_end(pe)

                phase_begin(pe, 2 * l + 2)
                E = EXPERTS[l]

                def norm_work(kind, b, c):
                    n = W[kind, b, c]
                    if n > 0:
                        pe.wait_ge(norm_free, n)
                    if kind == "ln":
                        pe.wait_ge(xn_ready, 4 * (8 * l + 4 + b + 1))
                        rows = 128 if c < 2 else 96
                        for t in range(TT):
                            ins = pe.transpose(ps[0:rows, 7, 128 * t:128 * t + 128], xn[:, t, 128 * c:128 * c + rows], ident[:, :])
                    else:
                        pe.wait_ge(hm_ready, 3 * (4 * l + b) + 3)
                        pe.wait_ge(wg_split, 3)
                        for t in range(TT):
                            ins = seven(ps[:, 7, 4 * t:4 * t + 4], lambda w, h, r: HM[0:r, b, h, 128 * t:128 * t + 128],
                                        lambda w, h, r: Wg[0:r, w, :])
                    ins.then_inc(norm_full, 1)

                def hidden(e, b, ft):
                    n, k = FT * (B * (EBASE[l] + e) + b) + ft, (EBASE[l] + e) % 2
                    if ft == 0:
                        pe.wait_ge(hm_ready, 3 * (4 * l + b) + 3)
                        pe.wait_ge(w_split, 12 * (EBASE[l] + e) + 6)
                    if n >= 3:
                        pe.wait_ge(f_free, n - 2)
                    seven(ps[:, 4 + n % 3, :], lambda w, h, r: W1[0:r, k, w, 128 * ft:128 * ft + 128],
                          lambda w, h, r: HM[0:r, b, h, :]).then_inc(f_full, 1)

                def back(e, b, ft):
                    U, k = B * (EBASE[l] + e) + b, (EBASE[l] + e) % 2
                    n = FT * U + ft
                    pe.wait_ge(g_ready, 2 * (n + 1))
                    if ft == 0:
                        pe.wait_ge(w_split, 12 * (EBASE[l] + e) + 12)
                    for t in range(TT):
                        if ft == 0 and U > 0:
                            pe.wait_ge(acc_free, TT * (U - 1) + t + 1)
                        for p, (x, w) in enumerate(((0, 0), (1, 0), (0, 1))):
                            ins = mm(ps[:, t, 0:C], G[:, n % 3, x, 128 * t:128 * t + 128], W2[:, k, w, ft, :],
                                     start=ft == 0 and p == 0, stop=ft == FT - 1 and p == 2)
                        if ft == FT - 1:
                            ins.then_inc(acc_full, 1)
                    if ft < FT - 1:
                        ins.then_inc(g_used, 1)

                for c in range(3):
                    norm_work("ln", 0, c)
                tiles = [(e, b, ft) for e in range(E) for b in range(B) for ft in range(FT)]
                for v, (e, b, ft) in enumerate(tiles):
                    if e == 0:
                        for key in norm_plan(l, b, ft):
                            norm_work(*key)
                    hidden(e, b, ft)
                    if v >= 2:
                        back(*tiles[v - 2])
                back(*tiles[-2])
                back(*tiles[-1])
                phase_end(pe)


BACKGROUND = sorted(
    [(3 + i, "skew", max(1, 7 * i), 7 * (i + 1) if i < 8 else D) for i in range(9)] + [(12, "turn")] +
    [(14 + i + i // 5, "exp", i // 2, i % 2) for i in range(2 * ROUNDS)] +
    [(13 + 3 * b + c + b, "x", b, c) for b in range(B) for c in range(3)] +
    [(16 + 4 * b, "y", b) for b in range(B)] +
    [(33 + 10 * l + i, "ada", l, i) for l in range(LAYERS) for i in range(10)], key=lambda x: x[0])

_INS = (["x", "P", "PT", "Wsk", "bsk", "cond", "ada_bcol", "ada_brow", "ada_w", "w_qkv", "w_proj", "qkcol", "vrow",
         "prow", "qkrow", "w_gate"] + [f"{n}_{l}" for l in range(LAYERS) for n in ("w1", "b1", "w2", "b2")])


def layout(inputs):
    g = {k: np.asarray(v) for k, v in inputs.items()}
    L = (dict(ada="L1_cond_W_ada", ba="L1_cond_b_ada", wq="L1_cond_W_qkv", bq="L1_cond_b_qkv", wp="L1_cond_W_proj",
              bp="L1_cond_b_proj", w1="L1_cond_W_fc1", b1="L1_cond_b_fc1", w2="L1_cond_W_fc2", b2="L1_cond_b_fc2"),
         dict(ada="L2_cond_w_ada", ba="L2_cond_b_ada", wq="L2_cond_w_qkv", bq="L2_cond_b_qkv", wp="L2_cond_w_proj",
              bp="L2_cond_b_proj", w1="L2_cond_w1", b1="L2_cond_b1", w2="L2_cond_w2", b2="L2_cond_b2"),
         dict(ada="L3_cond_w_adaln", ba="L3_cond_b_adaln", wq="L3_cond_w_qkv", bq="L3_cond_b_qkv",
              wp="L3_cond_w_proj", bp="L3_cond_b_proj", w1="L3_cond_w1", b1="L3_cond_b1", w2="L3_cond_w2",
              b2="L3_cond_b2"))
    f32 = np.float32
    o = {"x": g["x"], "P": g["L0_cond_P"], "PT": g["L0_cond_P"].T}
    iu, ju = np.triu_indices(D, k=1)
    by_column = np.lexsort((iu, ju))
    o["Wsk"] = g["L0_cond_W"][by_column].T
    o["bsk"] = np.zeros((D, D), f32)
    o["bsk"][iu, ju] = g["L0_cond_b"]
    o["cond"] = np.zeros((128, 3, B), f32)
    for c, rows in enumerate((128, 128, 32)):
        o["cond"][:rows, c, :] = g["cond_1152"].T[128 * c:128 * c + rows]
    heads = np.array([HD * h + d for h in ORDER for d in range(HD)])
    o["ada_bcol"] = np.zeros((128, LAYERS, 3, 4), f32)
    o["ada_brow"] = np.zeros((LAYERS, 2, C), f32)
    o["ada_w"] = np.zeros((LAYERS, C, 6 * C), f32)
    o["w_qkv"] = np.zeros((LAYERS, C, 3 * C), f32)
    o["w_proj"] = np.zeros((LAYERS, 128, 4, C), f32)
    o["qkcol"] = np.zeros((LAYERS, 126, 2, NM, 2), f32)
    o["vrow"] = np.zeros((LAYERS, C), f32)
    o["prow"] = np.zeros((LAYERS, C), f32)
    o["qkrow"] = np.zeros((LAYERS, 2, C), f32)
    for l in range(LAYERS):
        n = L[l]
        six = g[n["ba"]].reshape(6, C)
        for v, k in enumerate((0, 1, 3, 4)):
            for c in range(2):
                o["ada_bcol"][:, l, c, v] = six[k, 128 * c:128 * c + 128]
            for r in range(3):
                o["ada_bcol"][32 * r:32 * r + 32, l, 2, v] = six[k, 256:]
        o["ada_brow"][l, 0], o["ada_brow"][l, 1] = six[2], six[5]
        o["ada_w"][l] = g[n["ada"]]
        wq, bq = g[n["wq"]], g[n["bq"]]
        o["w_qkv"][l, :, :2 * C] = wq[:, :2 * C]
        o["w_qkv"][l, :, 2 * C:] = wq[:, 2 * C:][:, heads]
        o["vrow"][l] = bq[2 * C:][heads]
        for i, h in enumerate(ORDER):
            o["w_proj"][l, 32 * (i % 4):32 * (i % 4) + HD, i // 4, :] = g[n["wp"]][HD * h:HD * h + HD]
        o["prow"][l] = g[n["bp"]]
        for qk in range(2):
            for m in range(NM):
                r = MROWS[m]
                if l == 1:
                    o["qkcol"][l, :r, qk, m, 0] = np.tile(g["L2_cond_qn_g" if qk == 0 else "L2_cond_kn_g"], r // HD)
                    o["qkcol"][l, :r, qk, m, 1] = np.tile(g["L2_cond_qn_b" if qk == 0 else "L2_cond_kn_b"], r // HD)
                else:
                    o["qkcol"][l, :r, qk, m, 1] = bq[C * qk + 126 * m:C * qk + 126 * m + r]
            o["qkrow"][l, qk] = bq[C * qk:C * qk + C]
        E = EXPERTS[l]
        o[f"w1_{l}"] = g[n["w1"]].reshape(E, C, FF)
        o[f"w2_{l}"] = g[n["w2"]].reshape(E, FF, C)
        o[f"b1_{l}"] = g[n["b1"]].reshape(E, FT, 128).transpose(2, 0, 1)
        o[f"b2_{l}"] = g[n["b2"]].reshape(E, C)
    o["w_gate"] = g["L3_cond_w_gate"]
    return {k: np.ascontiguousarray(v) for k, v in o.items()}


def kernel(**inputs):
    import concourse.bacc as bacc
    from concourse.bass_utils import run_bass_kernel_spmd

    nc = bacc.Bacc("TRN2", target_bir_lowering=False, num_devices=1)
    data = layout(inputs)
    arrays = {f"in_{k}": data[k] for k in _INS}
    aps = {k: nc.dram_tensor(f"in_{k}", data[k].shape, F32, kind="ExternalInput").ap() for k in _INS}
    result = nc.dram_tensor("out_0", (B, N, C), F32, kind="ExternalOutput").ap()
    build(nc, aps, result)
    r = run_bass_kernel_spmd(nc, [arrays], core_ids=[0])
    return r.results[0]["out_0"]
```
